# Optimizing a Trainium2 kernel written in Bass

```python
import numpy as np
import jax
import jax.numpy as jnp

def _softmax(x, axis=-1):
    return jax.nn.softmax(x, axis=axis)

def _gelu(x):
    return jax.nn.gelu(x, approximate=True)

def _silu(x):
    return jax.nn.silu(x)

def _sigmoid(x):
    return jax.nn.sigmoid(x)

def _layernorm(x, axis=-1, eps=1e-05):
    m = jnp.mean(x, axis=axis, keepdims=True)
    v = jnp.var(x, axis=axis, keepdims=True)
    return (x - m) / jnp.sqrt(v + eps)

def _scatter_add(tgt, idx, src, axis=0):
    return tgt.at[idx].add(src)

def _segment_sum(src, seg, n):
    return jax.ops.segment_sum(src, seg, n)
kernel_name = 'mk_xattn_ffn_d1_seqx_r4_3dc5dc'

def setup_inputs(seed: int=0):
    np.random.seed(seed)
    _w = jnp.asarray

    def _rec_inputs():
        import jax
        import jax.numpy as jnp
        _rk = jax.random.key(seed)
        x = -0.000125 + 0.9999 * jax.random.normal(jax.random.fold_in(_rk, 1), (16, 128, 512), jnp.float32)
        _lenS = 128 - jax.random.randint(jax.random.fold_in(_rk, 7), (16,), 0, max(1, 128 // 4) + 1, jnp.int32)
        _lenS2 = 128 - jax.random.randint(jax.random.fold_in(_rk, 8), (16,), 0, max(1, 128 // 4) + 1, jnp.int32)
        _ctx_2048P = jax.random.normal(jax.random.fold_in(_rk, 11), (16, 16, 512), jnp.float32)
        _ctx_2048c = jax.random.dirichlet(jax.random.fold_in(_rk, 511), 0.3 * jnp.ones((16,), jnp.float32), (16, 128))
        _ctx_2048t = jnp.einsum('bsk,bkd->bsd', _ctx_2048c, _ctx_2048P)
        _ctx_2048t = _ctx_2048t * jax.lax.rsqrt(jnp.mean(jnp.square(_ctx_2048t)) + 1e-12) * 0.953939
        ctx_2048 = -0.000514642 + 1.00011 * (_ctx_2048t + 0.3 * jax.random.normal(jax.random.fold_in(_rk, 611), (16, 128, 512), jnp.float32))
        _validS = jnp.arange(128)[None, :] < _lenS[:, None]
        _validS2 = jnp.arange(128)[None, :] < _lenS2[:, None]
        _causal = jnp.tril(jnp.ones((128, 128), dtype=bool))
        mask_BxS2_bk0 = jnp.logical_not(jnp.broadcast_to(_validS2[:, :], (16, 128)))
        return (x, ctx_2048, mask_BxS2_bk0)
    x, ctx_2048, mask_BxS2_bk0 = _rec_inputs()

    def _L0_xattn_setup():
        import jax, jax.numpy as jnp
        import numpy as np
        key = jax.random.key(seed)
        k1, k2, k3 = jax.random.split(key, 3)
        B, S, D, M = (8, 512, 512, 128)
        hidden_states = jax.random.normal(k1, (B, S, D), dtype=jnp.float32)
        memory_tokens = jax.random.normal(k2, (B, M, D), dtype=jnp.float32)
        memory_mask = jax.random.randint(k3, (B, M), 0, 2).astype(jnp.bool_)
        return {'hidden_states': hidden_states, 'memory_tokens': memory_tokens, 'memory_mask': memory_mask}
    _L0_xattn_all = _L0_xattn_setup()
    _L0_xattn_in = {k: v for k, v in _L0_xattn_all.items() if k in ()}
    del _L0_xattn_all

    def _L0_ffn_setup():
        import jax, jax.numpy as jnp
        import numpy as np
        TOP_K = 2

        def moe_forward(x, w_gate_router, w_gate_proj, w_up_proj, w_down_proj):
            E = w_gate_router.shape[0]
            scores = jnp.einsum('bsd,ed->bse', x, w_gate_router)
            topk_scores, topk_idx = jax.lax.top_k(scores, TOP_K)
            topk_probs = jax.nn.softmax(topk_scores, axis=-1)
            weights = jnp.sum(topk_probs[..., None] * jax.nn.one_hot(topk_idx, E, dtype=x.dtype), axis=-2)
            gate = jnp.einsum('bsd,efd->bsef', x, w_gate_proj)
            up = jnp.einsum('bsd,efd->bsef', x, w_up_proj)
            hidden = jax.nn.silu(gate) * up
            out = jnp.einsum('bsef,edf,bse->bsd', hidden, w_down_proj, weights)
            return out
        key = jax.random.key(seed)
        k1, k2, k3, k4, k5 = jax.random.split(key, 5)
        B, S, D, E, F = (2, 256, 512, 8, 192)
        scale_in = 1.0 / np.sqrt(D)
        scale_ff = 1.0 / np.sqrt(F)
        return {'x': jax.random.normal(k1, (B, S, D), dtype=jnp.float32), 'w_gate_router': jax.random.normal(k2, (E, D), dtype=jnp.float32) * scale_in, 'w_gate_proj': jax.random.normal(k3, (E, F, D), dtype=jnp.float32) * scale_in, 'w_up_proj': jax.random.normal(k4, (E, F, D), dtype=jnp.float32) * scale_in, 'w_down_proj': jax.random.normal(k5, (E, D, F), dtype=jnp.float32) * scale_ff}
    _L0_ffn_all = _L0_ffn_setup()
    _L0_ffn_in = {k: v for k, v in _L0_ffn_all.items() if k in ('w_gate_router', 'w_gate_proj', 'w_up_proj', 'w_down_proj')}
    del _L0_ffn_all
    return {'x': x, 'ctx_2048': ctx_2048, 'mask_BxS2_bk0': mask_BxS2_bk0, 'L0_ffn_w_gate_router': _L0_ffn_in['w_gate_router'], 'L0_ffn_w_gate_proj': _L0_ffn_in['w_gate_proj'], 'L0_ffn_w_up_proj': _L0_ffn_in['w_up_proj'], 'L0_ffn_w_down_proj': _L0_ffn_in['w_down_proj']}

def reference(x, ctx_2048, mask_BxS2_bk0, L0_ffn_w_gate_router, L0_ffn_w_gate_proj, L0_ffn_w_up_proj, L0_ffn_w_down_proj):
    import jax
    import jax.numpy as jnp

    def _L0_xattn_ref(hidden_states, memory_tokens, memory_mask):
        import jax, jax.numpy as jnp
        import numpy as np
        B, S, D = hidden_states.shape
        scale = 1.0 / jnp.sqrt(jnp.asarray(D, hidden_states.dtype))
        scores = jnp.einsum('bsd,bmd->bsm', hidden_states, memory_tokens) * scale
        neg_inf = jnp.asarray(-1e+30, scores.dtype)
        scores = jnp.where(memory_mask[:, None, :], scores, neg_inf)
        attn = jax.nn.softmax(scores, axis=-1)
        readout = jnp.einsum('bsm,bmd->bsd', attn, memory_tokens)
        valid_b = jnp.any(memory_mask, axis=-1)
        out = jnp.where(valid_b[:, None, None], readout, jnp.zeros_like(readout))
        return out

    def _L0_ffn_ref(x, w_gate_router, w_gate_proj, w_up_proj, w_down_proj):
        import jax, jax.numpy as jnp
        import numpy as np
        TOP_K = 2

        def moe_forward(x, w_gate_router, w_gate_proj, w_up_proj, w_down_proj):
            E = w_gate_router.shape[0]
            scores = jnp.einsum('bsd,ed->bse', x, w_gate_router)
            topk_scores, topk_idx = jax.lax.top_k(scores, TOP_K)
            topk_probs = jax.nn.softmax(topk_scores, axis=-1)
            weights = jnp.sum(topk_probs[..., None] * jax.nn.one_hot(topk_idx, E, dtype=x.dtype), axis=-2)
            gate = jnp.einsum('bsd,efd->bsef', x, w_gate_proj)
            up = jnp.einsum('bsd,efd->bsef', x, w_up_proj)
            hidden = jax.nn.silu(gate) * up
            out = jnp.einsum('bsef,edf,bse->bsd', hidden, w_down_proj, weights)
            return out
        return moe_forward(x, w_gate_router, w_gate_proj, w_up_proj, w_down_proj)
    x = x + _L0_xattn_ref(_layernorm(x, axis=-1), ctx_2048, mask_BxS2_bk0)
    x = x + _L0_ffn_ref(_layernorm(x, axis=-1), L0_ffn_w_gate_router, L0_ffn_w_gate_proj, L0_ffn_w_up_proj, L0_ffn_w_down_proj)
    return x

_drawn_inputs = setup_inputs


def setup_inputs(seed=0):
    import zlib

    import numpy as np

    out = dict(_drawn_inputs(seed))
    spreads = {}
    factors = {}
    for name, (base, spread) in spreads.items():
        noise = np.random.default_rng([zlib.crc32(name.encode()), seed]).standard_normal(out[name].shape)
        drawn = base * np.exp(spread * noise) if base else spread * noise
        out[name] = jnp.asarray(drawn.astype(out[name].dtype))
    for name, factor in factors.items():
        out[name] = (out[name] * factor).astype(out[name].dtype)
    return out
```

```python
from contextlib import ExitStack

import concourse.bass as bass
from concourse import mybir

ALU = mybir.AluOpType
ACT = mybir.ActivationFunctionType
AX = mybir.AxisListType
F32 = mybir.dt.float32
F32R = mybir.dt.float32r
F16 = mybir.dt.float16
I32 = mybir.dt.int32
U32 = mybir.dt.uint32

P = 128
EPS = 1e-5
TOP_K = 2
MASKED = -1e30
LOWEST = -3e38


def xattn_moe_kernel(nc, x, ctx_tokens, mask, router_t, weights, out):
    B, S, D = x.shape
    E = router_t.shape[2]
    KD = D // P
    F = 192
    FB = F - P
    T = B * S
    NBLK = (TOP_K * T + E * (P - 1)) // P
    NA = TOP_K * B
    WGU = KD * 2 * F
    WA0 = E * WGU
    WB0 = WA0 + E * D
    WALL = WB0 + E // 2 * D
    WCH = WALL // B
    SCALE = float(D) ** -0.5
    assert S == P and FB == P // 2 and E * B == P and WALL == weights.shape[0] * weights.shape[2]

    xn2_rows = nc.dram_tensor("xn2_rows", (T, D), F32).ap()
    y_rows = nc.dram_tensor("y_rows", (NBLK * P, D), F32).ap()

    with ExitStack() as ctx:
        def sem(name):
            return ctx.enter_context(nc.semaphore(name))

        def sb(name, shape, dt, scope=ctx):
            return scope.enter_context(nc.sbuf_tensor(name, shape, dt))

        def ps(name, shape, dt, scope=ctx):
            return scope.enter_context(nc.psum_tensor(name, shape, dt))

        w_hi = sb("w_hi", [P, WALL], F32R)
        w_lo = sb("w_lo", [P, WALL], F32R)
        x1 = sb("x1", [P, B, D], F32)
        ident = sb("ident", [P, P], F32)
        row_iota = sb("row_iota", [P, P], F32)
        blk_iota = sb("blk_iota", [P, NBLK], F32)
        token_id = sb("token_id", [P, B], F32)
        expert_iota = sb("expert_iota", [P, B, E], F32)
        before_expert = sb("before_expert", [P, E, E], F32)
        before_token = sb("before_token", [P, P], F16)
        before_batch = sb("before_batch", [P, B, E], F16)
        same_expert = sb("same_expert", [P, E], F16)
        ones16 = sb("ones16", [P, P], F16)
        minus_half = sb("minus_half", [P, 1], F32)
        eps_col = sb("eps_col", [P, 1], F32)
        valid = sb("valid", [P, B], F32)
        gate1 = sb("gate1", [P, B], F32)
        gate2 = sb("gate2", [P, B], F32)
        slot_u = sb("slot_u", [P, NA], U32)
        slot_token = sb("slot_token", [P, NBLK], U32)
        blk_expert = sb("blk_expert", [P, NBLK], I32)
        blk_parity = sb("blk_parity", [P, 2, NBLK], F32)

        with ExitStack() as a:
            ctx_in = sb("ctx_in", [P, 4, D], F32, a)
            xn = sb("xn", [P, D], F32, a)
            xn_t = sb("xn_t", [P, KD, P], F32, a)
            ctx_t = sb("ctx_t", [P, KD, P], F32, a)
            mask_words = sb("mask_words", [P, B, P // 4], I32, a)
            bias = sb("bias", [P, 2, P], F32, a)
            scores = sb("scores", [P, P], F32, a)
            probs = sb("probs", [P, P], F32, a)
            probs_t = sb("probs_t", [P, P], F32, a)
            xn2 = sb("xn2", [P, 2, D], F32, a)
            xn2_t = sb("xn2_t", [P, KD, P], F32, a)
            router_w = sb("router_w", [P, KD, E], F32, a)
            w_stage = sb("w_stage", [P, 2, WCH], F32, a)
            bn_a = sb("bn_a", [P, 6], F32, a)
            bn_b = sb("bn_b", [P, 6], F32, a)
            mv1 = sb("mv1", [P, 2, 2], F32, a)
            mv2 = sb("mv2", [P, 2, 2], F32, a)
            var1 = sb("var1", [P, 1], F32, a)
            var2 = sb("var2", [P, 1], F32, a)
            rstd1 = sb("rstd1", [P, 1], F32, a)
            rstd2 = sb("rstd2", [P, 1], F32, a)
            top = sb("top", [P, 1], F32, a)
            neg_top = sb("neg_top", [P, 1], F32, a)
            psum_p = sb("psum_p", [P, 1], F32, a)
            inv_p = sb("inv_p", [P, 1], F32, a)
            factor = sb("factor", [P, 2, 1], F32, a)
        mask_u8 = mask_words[:, :, :].bitcast(mybir.dt.uint8)
        with ExitStack() as b:
            rs = sb("rs", [P, B, E], F32, b)
            rs2 = sb("rs2", [P, B, E], F32, b)
            not_top = sb("not_top", [P, B, E], F32, b)
            cand = sb("cand", [P, B, E], F32, b)
            top1 = sb("top1", [P, B], F32, b)
            top2 = sb("top2", [P, B], F32, b)
            first1 = sb("first1", [P, B], F32, b)
            first2 = sb("first2", [P, B], F32, b)
            hot1 = sb("hot1", [P, B, E], F32, b)
            hot2 = sb("hot2", [P, B, E], F32, b)
            hot16 = sb("hot16", [P, B, E], F16, b)
            exp_d = sb("exp_d", [P, B], F32, b)
            gap = sb("gap", [P, B], F32, b)
            denom = sb("denom", [P, B], F32, b)
            totals = sb("totals", [P, P], F16, b)
            blocks_i = sb("blocks_i", [P, 2, E], I32, b)
            blocks_f = sb("blocks_f", [P, E], F32, b)
            start_terms = sb("start_terms", [P, E, E], F32, b)
            start = sb("start", [P, E], F32, b)
            slot = sb("slot", [P, B, E], F32, b)
            picked = sb("picked", [P, 2, B, E], F32, b)
            slot_f = sb("slot_f", [P, NA], F32, b)
            slot_i = sb("slot_i", [P, 3, NA], I32, b)
            slot_hl = sb("slot_hl", [P, 2, NA], F32, b)
            begun = sb("begun", [P, NBLK, E - 1], F32, b)
            blk_f = sb("blk_f", [P, NBLK], F32, b)
            blk_odd = sb("blk_odd", [P, NBLK], I32, b)
            hot_row = sb("hot_row", [P, NA, P], F16, b)
            hot_blk = sb("hot_blk", [P, NA, NBLK], F16, b)
        with ExitStack() as c:
            idx = [sb(f"idx{u}", [P, 1], U32, c) for u in range(2)]
            xg = sb("xg", [P, 2, D], F32, c)
            xg_hi = sb("xg_hi", [P, 2, KD, P], F32R, c)
            xg_lo = sb("xg_lo", [P, 2, KD, P], F32R, c)
            act_g = sb("act_g", [P, 2, F], F32, c)
            hid = sb("hid", [P, 2, 2, P], F32, c)
            hid_hi = sb("hid_hi", [P, 2, 2, P], F32R, c)
            hid_lo = sb("hid_lo", [P, 2, 2, P], F32R, c)
            y = sb("y", [P, 2, D], F32, c)
        with ExitStack() as d:
            idx_d = [sb(f"idx_d{u}", [P, 1], U32, d) for u in range(4)]
            y1 = sb("y1", [P, 4, D], F32, d)
            y2 = sb("y2", [P, 4, D], F32, d)

        with ExitStack() as a:
            ps_x = ps("ps_x", [P, KD, P], F32, a)
            ps_c = ps("ps_c", [P, KD, P], F32, a)
            ps_s = ps("ps_s", [P, 512], F32, a)
            ps_p = ps("ps_p", [P, 512], F32, a)
            ps_r = ps("ps_r", [P, 2, 512], F32, a)
            ps_x2 = ps("ps_x2", [P, KD, P], F32, a)
            ps_router = ps("ps_router", [P, B * E], F32, a)
        with ExitStack() as b:
            ps_total = ps("ps_total", [P, 512], F32, b)
            ps_rank = ps("ps_rank", [P, 512], F32, b)
            ps_count = ps("ps_count", [P, 512], F32, b)
            ps_inv = ps("ps_inv", [P, 512], F32, b)
        with ExitStack() as c:
            ps_xg = ps("ps_xg", [P, 2, KD, P], F32, c)
            ps_gu = ps("ps_gu", [P, 2, 512], F32, c)
            ps_h = ps("ps_h", [P, 2, 512], F32, c)
            ps_y = ps("ps_y", [P, 2, 512], F32, c)

        const_made = sem("const_made")
        same_made = sem("same_made")
        batch_made = sem("batch_made")
        mask_loaded = sem("mask_loaded")
        router_loaded = sem("router_loaded")
        xc_loaded = [sem(f"xc_loaded{u}") for u in range(4)]
        w_loaded = [sem(f"w_loaded{u}") for u in range(2)]
        w_hi_done = sem("w_hi_done")
        w_lo_done = sem("w_lo_done")
        valid_done = sem("valid_done")
        mask_copied = sem("mask_copied")
        bias_done = sem("bias_done")
        bn1_done = sem("bn1_done")
        mv1_done = sem("mv1_done")
        var1_done = sem("var1_done")
        rstd1_done = sem("rstd1_done")
        xn_done = sem("xn_done")
        x_turned = sem("x_turned")
        c_turned = sem("c_turned")
        xt_ready = sem("xt_ready")
        ct_ready = sem("ct_ready")
        scored = sem("scored")
        top_done = sem("top_done")
        neg_done = sem("neg_done")
        exp_done = sem("exp_done")
        inv_done = sem("inv_done")
        factor_done = sem("factor_done")
        p_turned = sem("p_turned")
        pt_ready = sem("pt_ready")
        read_out = sem("read_out")
        x1_done = sem("x1_done")
        bn2_done = sem("bn2_done")
        mv2_done = sem("mv2_done")
        var2_done = sem("var2_done")
        rstd2_done = sem("rstd2_done")
        xn2_done = sem("xn2_done")
        xn2_stored = [sem(f"xn2_stored{u}") for u in range(2)]
        x2_turned = sem("x2_turned")
        x2t_ready = sem("x2t_ready")
        routed = sem("routed")
        sort_step = sem("sort_step")
        hot16_done = sem("hot16_done")
        totaled = sem("totaled")
        totals_done = sem("totals_done")
        ranked = sem("ranked")
        gap_done = sem("gap_done")
        exp_d_done = sem("exp_d_done")
        hots_done = sem("hots_done")
        inverted = sem("inverted")
        slot_token_done = sem("slot_token_done")
        blk_done = sem("blk_done")
        idx_done = sem("idx_done")
        gathered = [sem(f"gathered{u}") for u in range(2)]
        g_turned = sem("g_turned")
        g_hi = sem("g_hi")
        g_lo = sem("g_lo")
        gate_up = sem("gate_up")
        silu_done = sem("silu_done")
        hid_done = sem("hid_done")
        h_turned = sem("h_turned")
        h_hi = sem("h_hi")
        h_lo = sem("h_lo")
        down = sem("down")
        y_done = sem("y_done")
        y_stored = [sem(f"y_stored{u}") for u in range(2)]
        idx_d_done = sem("idx_d_done")
        rows_in = [sem(f"rows_in{u}") for u in range(4)]
        half_done = sem("half_done")
        out_done = sem("out_done")
        out_stored = sem("out_stored")
        waits_alone = sem("waits_alone")

        block = ctx.enter_context(nc.Block())

        def over_batches(eng, step, ahead, behind):
            rounds = (B - ahead - behind) // 4
            for i in range(-ahead, behind):
                step(0, i)
            with eng.Fori(0, rounds) as r:
                for u in range(behind, behind + 4):
                    step(r, u)
            for i in range(behind + 4 * rounds, B + behind):
                step(0, i)

        def on(r, u, shift, n=B):
            return not isinstance(r, int) or 0 <= 4 * r + u + shift < n

        def over_blocks(eng, step, first, last):
            for i in range(first, 4):
                step(0, i)
            with eng.Fori(0, (NBLK - 5) // 2) as r:
                for u in range(4, 6):
                    step(r, u)
            for i in range(NBLK - 1, last):
                step(0, i)

        def has(r, u, shift):
            return not isinstance(r, int) or 0 <= u + shift < NBLK

        def wait_alone(eng, signal, value):
            eng.wait_ge(signal, value)
            eng.sem_inc(waits_alone, 1)

        @block.sync
        def _(sp):
            sp.dma_start(x1[:, 0, :], x[0]).then_inc(xc_loaded[0], 16)
            sp.dma_start(ctx_in[:, 0, :], ctx_tokens[0]).then_inc(xc_loaded[0], 16)
            sp.dma_start(mask_words[:, :, :], mask.partition_broadcast(P)).then_inc(mask_loaded, 16)
            for i in range(1, 4):
                sp.dma_start(x1[:, i, :], x[i]).then_inc(xc_loaded[i], 16)
                sp.dma_start(ctx_in[:, i, :], ctx_tokens[i]).then_inc(xc_loaded[i], 16)
                if i == 1:
                    sp.dma_start(router_w[:, :, :], router_t).then_inc(router_loaded, 16)
                if i <= 2:
                    sp.dma_start(w_stage[:, i - 1, :], weights[i - 1]).then_inc(w_loaded[i - 1], 16)

            def batch(r, u):
                i = 4 * r + u
                if on(r, u, 2):
                    sp.wait_ge(w_hi_done, i + 1)
                    sp.wait_ge(w_lo_done, i + 1)
                    sp.dma_start(w_stage[:, u % 2, :], weights[i + 2]).then_inc(w_loaded[u % 2], 16)
                if on(r, u, -1):
                    sp.wait_ge(xn2_done, i)
                    sp.dma_start(xn2_rows[bass.ds((i - 1) * P, P), :],
                                 xn2[:, (u - 1) % 2, :]).then_inc(xn2_stored[(u - 1) % 2], 16)
                if on(r, u, 4):
                    sp.wait_ge(read_out, i + 1)
                    sp.dma_start(x1[:, i + 4, :], x[i + 4]).then_inc(xc_loaded[u % 4], 16)
                    sp.dma_start(ctx_in[:, u % 4, :], ctx_tokens[i + 4]).then_inc(xc_loaded[u % 4], 16)

            for i in range(0, 4):
                batch(0, i)
            with sp.Fori(1, B // 4 - 1) as r:
                for u in range(4):
                    batch(r, u)
            for i in range(B - 4, B + 1):
                batch(0, i)

            def store_y(r, u):
                b = 2 * r + u
                sp.wait_ge(y_done, b + 1)
                sp.dma_start(y_rows[bass.ds(b * P, P), :], y[:, u % 2, :]).then_inc(y_stored[u % 2], 16)

            with sp.Fori(0, NBLK // 2) as r:
                for u in range(2):
                    store_y(r, u)
            store_y(0, NBLK - 1)

            with sp.Fori(0, B) as t:
                sp.wait_ge(out_done, t + 1)
                sp.dma_start(out[t], x1[:, t, :]).then_inc(out_stored, 16)
            sp.wait_ge(out_stored, 16 * B)

        @block.gpsimd
        def _(pool):
            g = nc.gpsimd
            g.memset(minus_half[:, :], -0.5)
            g.memset(eps_col[:, :], EPS).then_inc(const_made, 1)
            g.memset(ident[:, :], 0.0).then_inc(const_made, 1)
            pool.wait_ge(const_made, 2)
            g.affine_select(out=ident[:, :], in_=ident[:, :], compare_op=ALU.not_equal, fill=1.0, base=0,
                            pattern=[[-1, P]], channel_multiplier=1).then_inc(const_made, 1)
            pool.wait_ge(mask_loaded, 16)

            def batch(r, u):
                i = 4 * r + u
                if on(r, u, 1):
                    if on(r, u, -1):
                        pool.wait_ge(top_done, i)
                    g.tensor_copy(bias[:, (u + 1) % 2, :], mask_u8[:, i + 1, :]).then_inc(mask_copied, 1)
                    wait_alone(pool, mask_copied, i + 2)
                    g.tensor_scalar(bias[:, (u + 1) % 2, :], bias[:, (u + 1) % 2, :], -MASKED / SCALE,
                                    MASKED / SCALE, ALU.mult, ALU.add).then_inc(bias_done, 1)
                if on(r, u, 2):
                    pool.wait_ge(mv1_done, i + 3)
                    g.tensor_tensor(var1[:, :], mv1[:, u % 2, 1:2], eps_col[:, :], ALU.add).then_inc(var1_done, 1)
                    pool.wait_ge(var1_done, i + 3)
                    if on(r, u, 1):
                        pool.wait_ge(xn_done, i + 2)
                    g.tensor_tensor(rstd1[:, :], var1[:, :], minus_half[:, :], ALU.pow).then_inc(rstd1_done, 1)
                if on(r, u, -1):
                    pool.wait_ge(mv2_done, i)
                    g.tensor_tensor(var2[:, :], mv2[:, (u - 1) % 2, 1:2], eps_col[:, :],
                                    ALU.add).then_inc(var2_done, 1)
                    pool.wait_ge(var2_done, i)
                    if on(r, u, -2):
                        pool.wait_ge(xn2_done, i - 1)
                    g.tensor_tensor(rstd2[:, :], var2[:, :], minus_half[:, :], ALU.pow).then_inc(rstd2_done, 1)
                if on(r, u, 0):
                    pool.wait_ge(w_hi_done, i + 1)
                    g.tensor_tensor(w_lo[:, bass.ds(i * WCH, WCH)], w_stage[:, u % 2, :],
                                    w_hi[:, bass.ds(i * WCH, WCH)].bitcast(F32),
                                    ALU.subtract).then_inc(w_lo_done, 1)
                if isinstance(r, int) and u == 0:
                    sort_constants()

            def sort_constants():
                g.memset(ones16[:, :], 1.0).then_inc(const_made, 1)
                g.iota(row_iota[:, :], [[1, P]], base=0, channel_multiplier=0,
                       allow_small_or_imprecise_dtypes=True).then_inc(const_made, 1)
                g.iota(blk_iota[:, :], [[1, NBLK]], base=0, channel_multiplier=0,
                       allow_small_or_imprecise_dtypes=True).then_inc(const_made, 1)
                g.iota(token_id[:, :], [[P, B]], base=0, channel_multiplier=1,
                       allow_small_or_imprecise_dtypes=True).then_inc(const_made, 1)
                g.iota(expert_iota[:, :, :], [[0, B], [1, E]], base=0, channel_multiplier=0,
                       allow_small_or_imprecise_dtypes=True).then_inc(const_made, 1)
                g.memset(before_expert[:, :, :], 1.0).then_inc(const_made, 1)
                pool.wait_ge(const_made, 9)
                g.affine_select(out=before_expert[:, :, :], in_=before_expert[:, :, :], compare_op=ALU.is_gt,
                                fill=0.0, base=0, pattern=[[1, E], [-1, E]],
                                channel_multiplier=0).then_inc(const_made, 1)
                g.affine_select(out=before_token[:, :], in_=ones16[:, :], compare_op=ALU.is_gt,
                                fill=0.0, base=0, pattern=[[1, P]],
                                channel_multiplier=-1).then_inc(const_made, 1)
                pool.wait_ge(batch_made, 1)
                g.affine_select(out=before_batch[:, :, :], in_=before_batch[:, :, :], compare_op=ALU.is_gt,
                                fill=0.0, base=0, pattern=[[E, B], [0, E]],
                                channel_multiplier=-1).then_inc(batch_made, 1)

            over_batches(pool, batch, 2, 2)

            pool.wait_ge(slot_token_done, 1)
            pool.wait_ge(xn2_stored[0], 16 * (B // 2))
            pool.wait_ge(xn2_stored[1], 16 * (B // 2))

            def gather(r, u):
                b = 2 * r + u
                if has(r, u, -2):
                    pool.wait_ge(gathered[u % 2], 16 * r + 16 * ((u - 2) // 2 + 1))
                    pool.wait_ge(g_turned, b - 1)
                g.tensor_copy(idx[u % 2][:, :], slot_token[:, bass.ds(b, 1)]).then_inc(idx_done, 1)
                wait_alone(pool, idx_done, b + 1)
                g.indirect_dma_start(out=xg[:, u % 2, :], out_offset=None, in_=xn2_rows[:, :],
                                     in_offset=bass.IndirectOffsetOnAxis(ap=idx[u % 2][:, 0:1], axis=0)
                                     ).then_inc(gathered[u % 2], 16)

            over_blocks(pool, gather, 0, NBLK)

            pool.wait_ge(y_stored[0], 16 * ((NBLK + 1) // 2))
            pool.wait_ge(y_stored[1], 16 * (NBLK // 2))

            def fetch(r, u):
                t = 4 * r + u
                if not isinstance(r, int) or r:
                    pool.wait_ge(out_done, t - 3)
                    pool.wait_ge(rows_in[u], 32 * r)
                for k, rows in enumerate((y1, y2)):
                    j = 2 * (u % 2) + k
                    if not isinstance(r, int) or r or u >= 2:
                        pool.wait_ge(rows_in[(u - 2) % 4], 32 * r if u < 2 else 32 * r + 32)
                    g.tensor_copy(idx_d[j][:, :], slot_u[:, bass.ds(k * B + t, 1)]).then_inc(idx_d_done, 1)
                    wait_alone(pool, idx_d_done, 2 * t + k + 1)
                    g.indirect_dma_start(out=rows[:, u, :], out_offset=None, in_=y_rows[:, :],
                                         in_offset=bass.IndirectOffsetOnAxis(ap=idx_d[j][:, 0:1], axis=0)
                                         ).then_inc(rows_in[u], 16)

            for u in range(4):
                fetch(0, u)
            with pool.Fori(1, B // 4) as r:
                for u in range(4):
                    fetch(r, u)

        @block.tensor
        def _(pe):
            t = nc.tensor
            pe.wait_ge(const_made, 3)
            pe.wait_ge(router_loaded, 16)

            def batch(r, u):
                i = 4 * r + u
                if on(r, u, 0):
                    pe.wait_ge(xt_ready, i + 1)
                    pe.wait_ge(ct_ready, i + 1)
                    if on(r, u, -1):
                        pe.wait_ge(top_done, i)
                    for k in range(KD):
                        mm = t.matmul(ps_s[:, 0:P], xn_t[:, k, :], ctx_t[:, k, :],
                                      start=(k == 0), stop=(k == KD - 1))
                    mm.then_inc(scored, 1)
                if on(r, u, 1):
                    v = u + 1
                    pe.wait_ge(xc_loaded[v % 4], 32 * r + 32 * (v // 4 + 1))
                    if on(r, u, 0):
                        pe.wait_ge(ct_ready, i + 1)
                    for k in range(KD):
                        mm = t.transpose(ps_c[:, k, :], ctx_in[:, v % 4, k * P:(k + 1) * P], ident[:, :])
                    mm.then_inc(c_turned, 1)
                    pe.wait_ge(xn_done, i + 2)
                    for k in range(KD):
                        mm = t.transpose(ps_x[:, k, :], xn[:, k * P:(k + 1) * P], ident[:, :])
                    mm.then_inc(x_turned, 1)
                if on(r, u, -3):
                    pe.wait_ge(x2t_ready, i - 2)
                    for k in range(KD):
                        mm = t.matmul(ps_router[:, bass.ds((i - 3) * E, E)], xn2_t[:, k, :], router_w[:, k, :],
                                      start=(k == 0), stop=(k == KD - 1))
                    mm.then_inc(routed, 1)
                if on(r, u, 0):
                    pe.wait_ge(exp_done, i + 1)
                    t.transpose(ps_p[:, 0:P], probs[:, :], ident[:, :]).then_inc(p_turned, 1)
                if on(r, u, -2):
                    pe.wait_ge(xn2_done, i - 1)
                    for k in range(KD):
                        mm = t.transpose(ps_x2[:, k, :], xn2[:, u % 2, k * P:(k + 1) * P], ident[:, :])
                    mm.then_inc(x2_turned, 1)
                if on(r, u, 0):
                    pe.wait_ge(pt_ready, i + 1)
                    if on(r, u, -2):
                        pe.wait_ge(x1_done, i - 1)
                    t.matmul(ps_r[:, u % 2, :], probs_t[:, :], ctx_in[:, u % 4, :],
                             start=True, stop=True).then_inc(read_out, 1)

            over_batches(pe, batch, 1, 3)

            pe.wait_ge(hot16_done, 1)
            t.matmul(ps_total[:, 0:1], hot16.rearrange("p b e -> p (b e)"), ones16[:, 0:1],
                     start=True, stop=True).then_inc(totaled, 1)
            pe.wait_ge(totals_done, 1)
            pe.wait_ge(batch_made, 2)
            t.matmul(ps_count[:, 0:E], totals[:, :], same_expert[:, :], start=True, stop=True).then_inc(ranked, 1)
            pe.wait_ge(const_made, 11)
            t.matmul(ps_rank[:, 0:P], before_token[:, :], hot16.rearrange("p b e -> p (b e)"),
                     start=True, stop=False)
            t.matmul(ps_rank[:, 0:P], totals[:, :], before_batch.rearrange("p b e -> p (b e)"),
                     start=False, stop=True).then_inc(ranked, 1)
            for n in range(NA):
                pe.wait_ge(hots_done, 2 * n + 2)
                mm = t.matmul(ps_inv[:, 0:NBLK], hot_row[:, n, :], hot_blk[:, n, :],
                              start=(n == 0), stop=(n == NA - 1))
            mm.then_inc(inverted, 1)

            pe.wait_ge(w_hi_done, B)
            pe.wait_ge(w_lo_done, B)
            pe.wait_ge(blk_done, 1)
            pe.wait_ge(slot_token_done, 1)

            def expert_of(b):
                return pe.value_load(blk_expert[0:1, bass.ds(b, 1)], min_val=0, max_val=E - 1)

            def blocks(r, u):
                b = 2 * r + u
                if has(r, u, 0):
                    e = expert_of(b)
                if has(r, u, -2):
                    e_down = expert_of(b - 2)
                if has(r, u, 0):
                    pe.wait_ge(g_hi, b + 1)
                    pe.wait_ge(g_lo, b + 1)
                    if has(r, u, -2):
                        pe.wait_ge(hid_done, b - 1)
                    n = 0
                    for k in range(KD):
                        for lhs, w in ((xg_hi, w_hi), (xg_hi, w_lo), (xg_lo, w_hi)):
                            mm = t.matmul(ps_gu[:, u % 2, 0:2 * F], lhs[:, u % 2, k, :],
                                          w[:, bass.ds(e * WGU + k * 2 * F, 2 * F)],
                                          start=(n == 0), stop=(n == 3 * KD - 1))
                            n += 1
                    mm.then_inc(gate_up, 1)
                if has(r, u, 1):
                    v = u + 1
                    pe.wait_ge(gathered[v % 2], 16 * r + 16 * (v // 2 + 1))
                    if has(r, u, -1):
                        pe.wait_ge(g_lo, b)
                        pe.wait_ge(g_hi, b)
                    for k in range(KD):
                        mm = t.transpose(ps_xg[:, v % 2, k, :], xg[:, v % 2, k * P:(k + 1) * P], ident[:, :])
                    mm.then_inc(g_turned, 1)
                if has(r, u, -1):
                    v = u - 1
                    pe.wait_ge(hid_done, b)
                    if has(r, u, -3):
                        pe.wait_ge(h_hi, b - 2)
                        pe.wait_ge(h_lo, b - 2)
                    for half in range(2):
                        mm = t.transpose(ps_h[:, v % 2, half * P:(half + 1) * P], hid[:, v % 2, half, :], ident[:, :])
                    mm.then_inc(h_turned, 1)
                if has(r, u, -2):
                    pe.wait_ge(h_hi, b - 1)
                    pe.wait_ge(h_lo, b - 1)
                    if has(r, u, -4):
                        pe.wait_ge(y_done, b - 3)
                    n = 0
                    for half, base, row in ((0, WA0, e_down), (1, WB0, e_down // 2)):
                        for lhs, w in ((hid_hi, w_hi), (hid_hi, w_lo), (hid_lo, w_hi)):
                            mm = t.matmul(ps_y[:, u % 2, :], lhs[:, u % 2, half, :],
                                          w[:, bass.ds(row * D + base, D)],
                                          start=(n == 0), stop=(n == 5))
                            n += 1
                    mm.then_inc(down, 1)

            over_blocks(pe, blocks, -1, NBLK + 2)

        @block.scalar
        def _(act):
            s = nc.scalar

            def batch(r, u):
                i = 4 * r + u
                if on(r, u, 0):
                    pe_free = on(r, u, -1)
                    act.wait_ge(neg_done, i + 1)
                    if pe_free:
                        act.wait_ge(p_turned, i)
                    s.activation(probs[:, :], scores[:, :], ACT.Exp, bias=neg_top[:, :],
                                 accum_out=psum_p[:, :]).then_inc(exp_done, 1)
                if on(r, u, 1):
                    act.wait_ge(c_turned, i + 2)
                    if on(r, u, 0):
                        act.wait_ge(scored, i + 1)
                    s.activation(ctx_t[:, :, :], ps_c[:, :, :], ACT.Copy).then_inc(ct_ready, 1)
                    act.wait_ge(x_turned, i + 2)
                    s.activation(xn_t[:, :, :], ps_x[:, :, :], ACT.Copy).then_inc(xt_ready, 1)
                if on(r, u, 0):
                    act.wait_ge(p_turned, i + 1)
                    if on(r, u, -1):
                        act.wait_ge(read_out, i)
                    s.activation(probs_t[:, :], ps_p[:, 0:P], ACT.Copy).then_inc(pt_ready, 1)
                if on(r, u, -2):
                    act.wait_ge(x2_turned, i - 1)
                    if on(r, u, -3):
                        act.wait_ge(routed, i - 2)
                    s.activation(xn2_t[:, :, :], ps_x2[:, :, :], ACT.Copy).then_inc(x2t_ready, 1)
                if on(r, u, 0):
                    act.wait_ge(w_loaded[u % 2], 32 * r + 16 * (u // 2 + 1))
                    s.activation(w_hi[:, bass.ds(i * WCH, WCH)], w_stage[:, u % 2, :],
                                 ACT.Copy).then_inc(w_hi_done, 1)

            over_batches(act, batch, 1, 3)

            act.wait_ge(gap_done, 1)
            s.activation(exp_d[:, :], gap[:, :], ACT.Exp).then_inc(exp_d_done, 1)

            def blocks(r, u):
                b = 2 * r + u
                if has(r, u, 0):
                    act.wait_ge(gate_up, b + 1)
                    if has(r, u, -2):
                        act.wait_ge(hid_done, b - 1)
                    s.activation(act_g[:, u % 2, :], ps_gu[:, u % 2, 0:F], ACT.Silu).then_inc(silu_done, 1)
                if has(r, u, 1):
                    v = u + 1
                    act.wait_ge(g_turned, b + 2)
                    if has(r, u, -1):
                        act.wait_ge(gate_up, b)
                    s.activation(xg_hi[:, v % 2, :, :], ps_xg[:, v % 2, :, :], ACT.Copy).then_inc(g_hi, 1)
                if has(r, u, -1):
                    v = u - 1
                    act.wait_ge(h_turned, b)
                    if has(r, u, -3):
                        act.wait_ge(down, b - 2)
                    s.activation(hid_hi[:, v % 2, :, :], ps_h[:, v % 2, 0:2 * P],
                                 ACT.Copy).then_inc(h_hi, 1)
                if has(r, u, -2):
                    act.wait_ge(down, b - 1)
                    if has(r, u, -4):
                        act.wait_ge(y_stored[u % 2], 16 * r + 16 * ((u - 4) // 2 + 1))
                    s.activation(y[:, u % 2, :], ps_y[:, u % 2, :], ACT.Copy).then_inc(y_done, 1)

            over_blocks(act, blocks, -1, NBLK + 2)

        @block.vector
        def _(dve):
            v_ = nc.vector
            dve.wait_ge(const_made, 3)
            with nc.allow_low_precision("zeros and ones"):
                v_.tensor_reduce(same_expert[:, :], ident.rearrange("p (b e) -> p e b", e=E), AX.X,
                                 ALU.add).then_inc(same_made, 1)
            dve.wait_ge(same_made, 1)
            v_.tensor_copy(before_batch[:, :, :],
                           same_expert[:, :].unsqueeze(1).to_broadcast([P, B, E])).then_inc(batch_made, 1)

            def batch(r, u):
                i = 4 * r + u
                if on(r, u, 0):
                    if on(r, u, -1):
                        dve.wait_ge(exp_done, i)
                    dve.wait_ge(bias_done, i + 1)
                    wait_alone(dve, scored, i + 1)
                    v_.tensor_tensor_reduce(scores[:, :], ps_s[:, 0:P], bias[:, u % 2, :], SCALE, LOWEST,
                                            ALU.add, ALU.max, top[:, :]).then_inc(top_done, 1)
                    dve.wait_ge(top_done, i + 1)
                    v_.tensor_scalar(neg_top[:, :], top[:, :], -1.0, None, ALU.mult).then_inc(neg_done, 1)
                if on(r, u, -1):
                    v = u - 1
                    dve.wait_ge(read_out, i)
                    dve.wait_ge(factor_done, i)
                    v_.scalar_tensor_tensor(x1[:, i - 1, :], ps_r[:, v % 2, :], factor[:, v % 2, :],
                                            x1[:, i - 1, :], ALU.mult, ALU.add).then_inc(x1_done, 1)
                    wait_alone(dve, x1_done, i)
                    v_.bn_stats(bn_b[:, :], x1[:, i - 1, :]).then_inc(bn2_done, 1)
                    wait_alone(dve, bn2_done, i)
                    v_.bn_aggr(mv2[:, v % 2, :], bn_b[:, :]).then_inc(mv2_done, 1)
                if on(r, u, 0):
                    dve.wait_ge(exp_done, i + 1)
                    v_.reciprocal(inv_p[:, :], psum_p[:, :]).then_inc(inv_done, 1)
                    dve.wait_ge(inv_done, i + 1)
                    if isinstance(r, int) and u == 0:
                        dve.wait_ge(valid_done, 1)
                    v_.tensor_scalar(factor[:, u % 2, :], inv_p[:, :], valid[:, bass.ds(i, 1)], None,
                                     ALU.mult).then_inc(factor_done, 1)
                if on(r, u, 2):
                    dve.wait_ge(rstd1_done, i + 3)
                    if on(r, u, 1):
                        dve.wait_ge(x_turned, i + 2)
                    v_.tensor_scalar(xn[:, :], x1[:, i + 2, :], mv1[:, u % 2, 0:1], rstd1[:, :],
                                     ALU.subtract, ALU.mult).then_inc(xn_done, 1)
                if on(r, u, 3):
                    v = u + 3
                    wait_alone(dve, xc_loaded[v % 4], 32 * r + 32 * (v // 4 + 1))
                    v_.bn_stats(bn_a[:, :], x1[:, i + 3, :]).then_inc(bn1_done, 1)
                    wait_alone(dve, bn1_done, i + 4)
                    v_.bn_aggr(mv1[:, v % 2, :], bn_a[:, :]).then_inc(mv1_done, 1)
                if isinstance(r, int) and u == -1:
                    dve.wait_ge(mask_loaded, 16)
                    v_.tensor_reduce(valid[:, :], mask_u8, AX.X, ALU.max).then_inc(valid_done, 1)
                if on(r, u, -1):
                    dve.wait_ge(rstd2_done, i)
                    if on(r, u, -3):
                        dve.wait_ge(x2_turned, i - 2)
                        dve.wait_ge(xn2_stored[(u - 1) % 2], 32 * r + 16 * ((u - 3) // 2 + 1))
                    v_.tensor_scalar(xn2[:, (u - 1) % 2, :], x1[:, i - 1, :], mv2[:, (u - 1) % 2, 0:1],
                                     rstd2[:, :], ALU.subtract, ALU.mult).then_inc(xn2_done, 1)

            over_batches(dve, batch, 3, 3)

            chain = [0]

            def then(ins):
                chain[0] += 1
                ins.then_inc(sort_step, 1)
                dve.wait_ge(sort_step, chain[0])

            def over_e(m):
                return m.unsqueeze(2).to_broadcast([P, B, E])

            dve.wait_ge(routed, B)
            dve.wait_ge(xn2_stored[0], 16 * (B // 2))
            dve.wait_ge(xn2_stored[1], 16 * (B // 2))
            dve.wait_ge(const_made, 11)
            dve.wait_ge(batch_made, 2)
            then(v_.tensor_copy(rs[:, :, :], ps_router.rearrange("p (b e) -> p b e", e=E)))
            then(v_.tensor_reduce(top1[:, :], rs[:, :, :], AX.X, ALU.max))
            then(v_.tensor_tensor(not_top[:, :, :], rs[:, :, :], over_e(top1[:, :]), ALU.is_lt))
            then(v_.scalar_tensor_tensor(cand[:, :, :], not_top[:, :, :], float(E), expert_iota[:, :, :],
                                         ALU.mult, ALU.add))
            then(v_.tensor_reduce(first1[:, :], cand[:, :, :], AX.X, ALU.min))
            then(v_.tensor_tensor(hot1[:, :, :], expert_iota[:, :, :], over_e(first1[:, :]), ALU.is_equal))
            then(v_.scalar_tensor_tensor(rs2[:, :, :], hot1[:, :, :], LOWEST, rs[:, :, :], ALU.mult, ALU.add))
            then(v_.tensor_reduce(top2[:, :], rs2[:, :, :], AX.X, ALU.max))
            then(v_.tensor_tensor(not_top[:, :, :], rs2[:, :, :], over_e(top2[:, :]), ALU.is_lt))
            then(v_.scalar_tensor_tensor(cand[:, :, :], not_top[:, :, :], float(E), expert_iota[:, :, :],
                                         ALU.mult, ALU.add))
            then(v_.tensor_reduce(first2[:, :], cand[:, :, :], AX.X, ALU.min))
            then(v_.tensor_tensor(hot2[:, :, :], expert_iota[:, :, :], over_e(first2[:, :]), ALU.is_equal))
            v_.tensor_tensor(hot16[:, :, :], hot1[:, :, :], hot2[:, :, :], ALU.add).then_inc(hot16_done, 1)
            v_.tensor_tensor(gap[:, :], top2[:, :], top1[:, :], ALU.subtract).then_inc(gap_done, 1)
            dve.wait_ge(totaled, 1)
            v_.tensor_scalar(totals[:, :], ones16[:, :], ps_total[:, 0:1], None, ALU.mult).then_inc(totals_done, 1)
            dve.wait_ge(ranked, 1)
            then(v_.tensor_scalar(blocks_i[:, 0, :], ps_count[:, 0:E], float(P - 1), None, ALU.add))
            then(v_.tensor_scalar(blocks_i[:, 1, :], blocks_i[:, 0, :], 7, None, ALU.logical_shift_right))
            then(v_.tensor_copy(blocks_f[:, :], blocks_i[:, 1, :]))
            then(v_.tensor_tensor(start_terms[:, :, :], before_expert[:, :, :],
                                  blocks_f[:, :].unsqueeze(1).to_broadcast([P, E, E]), ALU.mult))
            then(v_.tensor_reduce(start[:, :], start_terms[:, :, :], AX.X, ALU.add))
            dve.wait_ge(ranked, 2)
            then(v_.scalar_tensor_tensor(slot[:, :, :], start[:, :].unsqueeze(1).to_broadcast([P, B, E]), float(P),
                                         ps_rank[:, 0:P].rearrange("p (b e) -> p b e", e=E),
                                         ALU.mult, ALU.add))
            v_.tensor_tensor(picked[:, 0, :, :], hot1[:, :, :], slot[:, :, :], ALU.mult)
            then(v_.tensor_tensor(picked[:, 1, :, :], hot2[:, :, :], slot[:, :, :], ALU.mult))
            then(v_.tensor_reduce(slot_f[:, :], picked.rearrange("p k b e -> p (k b) e"), AX.X, ALU.add))
            then(v_.tensor_copy(slot_i[:, 0, :], slot_f[:, :]))
            v_.tensor_scalar(slot_i[:, 1, :], slot_i[:, 0, :], 7, None, ALU.logical_shift_right)
            then(v_.tensor_scalar(slot_i[:, 2, :], slot_i[:, 0, :], P - 1, None, ALU.bitwise_and))
            then(v_.tensor_copy(slot_hl[:, :, :], slot_i[:, 1:3, :]))
            for n in range(NA):
                v_.tensor_scalar(hot_row[:, n, :], row_iota[:, :], slot_hl[:, 1, n:n + 1], None,
                                 ALU.is_equal).then_inc(hots_done, 1)
                v_.tensor_scalar(hot_blk[:, n, :], blk_iota[:, :], slot_hl[:, 0, n:n + 1],
                                 token_id[:, n % B:n % B + 1], ALU.is_equal, ALU.mult).then_inc(hots_done, 1)
            then(v_.tensor_tensor(begun[:, :, :], blk_iota[:, :].unsqueeze(2).to_broadcast([P, NBLK, E - 1]),
                                  start[:, 1:E].unsqueeze(1).to_broadcast([P, NBLK, E - 1]), ALU.is_ge))
            then(v_.tensor_reduce(blk_f[:, :], begun[:, :, :], AX.X, ALU.add))
            then(v_.tensor_copy(blk_expert[:, :], blk_f[:, :]))
            then(v_.tensor_scalar(blk_odd[:, :], blk_expert[:, :], 1, None, ALU.bitwise_and))
            then(v_.tensor_copy(blk_parity[:, 1, :], blk_odd[:, :]))
            v_.tensor_scalar(blk_parity[:, 0, :], blk_parity[:, 1, :], -1.0, 1.0, ALU.mult,
                             ALU.add).then_inc(blk_done, 1)
            dve.wait_ge(blk_done, 1)
            dve.wait_ge(exp_d_done, 1)
            then(v_.tensor_scalar(denom[:, :], exp_d[:, :], 1.0, None, ALU.add))
            then(v_.reciprocal(gate1[:, :], denom[:, :]))
            then(v_.tensor_tensor(gate2[:, :], gate1[:, :], exp_d[:, :], ALU.mult))
            then(v_.tensor_copy(slot_u[:, :], slot_f[:, :]))
            dve.wait_ge(inverted, 1)
            v_.tensor_copy(slot_token[:, :], ps_inv[:, 0:NBLK]).then_inc(slot_token_done, 1)

            def blocks(r, u):
                b = 2 * r + u
                if has(r, u, 0):
                    dve.wait_ge(silu_done, b + 1)
                    if has(r, u, -2):
                        dve.wait_ge(h_turned, b - 1)
                    v_.tensor_tensor(hid[:, u % 2, 0, :], act_g[:, u % 2, 0:P], ps_gu[:, u % 2, F:F + P],
                                     ALU.mult)
                    for odd in range(2):
                        last = v_.scalar_tensor_tensor(
                            hid[:, u % 2, 1, odd * FB:(odd + 1) * FB], act_g[:, u % 2, P:F],
                            blk_parity[:, odd, bass.ds(b, 1)], ps_gu[:, u % 2, F + P:2 * F],
                            ALU.mult, ALU.mult)
                    last.then_inc(hid_done, 1)
                if has(r, u, 1):
                    v = u + 1
                    dve.wait_ge(g_hi, b + 2)
                    v_.tensor_tensor(xg_lo[:, v % 2, :, :], ps_xg[:, v % 2, :, :],
                                     xg_hi[:, v % 2, :, :].bitcast(F32), ALU.subtract).then_inc(g_lo, 1)
                if has(r, u, -1):
                    v = u - 1
                    dve.wait_ge(h_hi, b)
                    v_.tensor_tensor(hid_lo[:, v % 2, :, :],
                                     ps_h[:, v % 2, 0:2 * P].rearrange("p (h t) -> p h t", h=2),
                                     hid_hi[:, v % 2, :, :].bitcast(F32), ALU.subtract).then_inc(h_lo, 1)

            over_blocks(dve, blocks, -1, NBLK + 1)

            def combine(r, u):
                t = 4 * r + u
                dve.wait_ge(rows_in[u], 32 * r + 32)
                v_.scalar_tensor_tensor(x1[:, t, :], y1[:, u, :], gate1[:, bass.ds(t, 1)], x1[:, t, :],
                                        ALU.mult, ALU.add).then_inc(half_done, 1)
                dve.wait_ge(half_done, t + 1)
                v_.scalar_tensor_tensor(x1[:, t, :], y2[:, u, :], gate2[:, bass.ds(t, 1)], x1[:, t, :],
                                        ALU.mult, ALU.add).then_inc(out_done, 1)

            with dve.Fori(0, B // 4) as r:
                for u in range(4):
                    combine(r, u)


def kernel(x, ctx_2048, mask_BxS2_bk0, L0_ffn_w_gate_router, L0_ffn_w_gate_proj, L0_ffn_w_up_proj,
           L0_ffn_w_down_proj):
    import numpy as np
    import concourse.bacc as bacc
    from concourse import mybir as mb
    from concourse.bass_utils import run_bass_kernel_spmd

    P = 128
    x, ctx_2048 = np.asarray(x), np.asarray(ctx_2048)
    router, gate, up, down = (np.asarray(a) for a in (L0_ffn_w_gate_router, L0_ffn_w_gate_proj,
                                                      L0_ffn_w_up_proj, L0_ffn_w_down_proj))
    B, S, D = x.shape
    E, F, _ = gate.shape
    KD = D // P
    gu = np.concatenate([gate.transpose(0, 2, 1), up.transpose(0, 2, 1)], axis=2)
    gu = gu.reshape(E, KD, P, 2 * F).transpose(2, 0, 1, 3).reshape(P, -1)
    dn = down.transpose(0, 2, 1)
    first = dn[:, :P].transpose(1, 0, 2).reshape(P, -1)
    rest = dn[:, P:].reshape(E // 2, 2, F - P, D).transpose(1, 2, 0, 3).reshape(P, -1)
    w = np.concatenate([gu, first, rest], axis=1)
    w = w.reshape(P, B, -1).transpose(1, 0, 2)
    arrays = {
        "x": x,
        "ctx": ctx_2048,
        "mask": np.ascontiguousarray(mask_BxS2_bk0).view(np.int32),
        "router_t": router.transpose(1, 0).reshape(KD, P, E).transpose(1, 0, 2),
        "weights": w,
    }
    arrays = {k: np.ascontiguousarray(v) for k, v in arrays.items()}
    nc = bacc.Bacc("TRN2", target_bir_lowering=False, num_devices=1, dynamic_dma_scratch_size=8192)
    args = [nc.dram_tensor(k, v.shape, mb.dt.from_np(v.dtype), kind="ExternalInput").ap()
            for k, v in arrays.items()]
    out = nc.dram_tensor("out", (B, S, D), mb.dt.float32, kind="ExternalOutput").ap()
    xattn_moe_kernel(nc, *args, out)
    got = run_bass_kernel_spmd(nc, [arrays], core_ids=[0])
    return got.results[0]["out"]
```

```python
from contextlib import ExitStack

import concourse.bass as bass
from concourse import mybir

ALU = mybir.AluOpType
ACT = mybir.ActivationFunctionType
AX = mybir.AxisListType
F32 = mybir.dt.float32
F32R = mybir.dt.float32r
F16 = mybir.dt.float16
I32 = mybir.dt.int32
U32 = mybir.dt.uint32

P = 128
EPS = 1e-5
TOP_K = 2
MASKED = -1e30
LOWEST = -3e38


def xattn_moe_kernel(nc, x, ctx_tokens, mask, router_t, weights, out):
    B, S, D = x.shape
    E = router_t.shape[2]
    KD = D // P
    F = 192
    FB = F - P
    T = B * S
    NBLK = (TOP_K * T + E * (P - 1)) // P
    NA = TOP_K * B
    WGU = KD * 2 * F
    WA0 = E * WGU
    WB0 = WA0 + E * D
    WALL = WB0 + E // 2 * D
    WCH = WALL // B
    SCALE = float(D) ** -0.5
    CHUNK = 4
    assert S == P and FB == P // 2 and E * B == P and WALL == weights.shape[0] * weights.shape[2]

    xn2_rows = nc.dram_tensor("xn2_rows", (T + P, D), F32).ap()

    with ExitStack() as ctx:
        def sem(name):
            return ctx.enter_context(nc.semaphore(name))

        def sb(name, shape, dt, scope=ctx):
            return scope.enter_context(nc.sbuf_tensor(name, shape, dt))

        def ps(name, shape, dt, scope=ctx):
            return scope.enter_context(nc.psum_tensor(name, shape, dt))

        w_hi = sb("w_hi", [P, WALL], F32R)
        w_lo = sb("w_lo", [P, WALL], F32R)
        x1 = sb("x1", [P, B, D], F32)
        ident = sb("ident", [P, P], F32)
        row_iota = sb("row_iota", [P, P], F32)
        blk_iota = sb("blk_iota", [P, NBLK], F32)
        token_off = sb("token_off", [P, TOP_K, B], F32)
        pad_token = sb("pad_token", [P, 1], F32)
        expert_iota = sb("expert_iota", [P, B, E], F32)
        before_expert = sb("before_expert", [P, E, E], F32)
        before_token = sb("before_token", [P, P], F16)
        before_batch = sb("before_batch", [P, B, E], F16)
        same_expert = sb("same_expert", [P, E], F16)
        ones16 = sb("ones16", [P, P], F16)
        minus_half = sb("minus_half", [P, 1], F32)
        eps_col = sb("eps_col", [P, 1], F32)
        valid = sb("valid", [P, B], F32)
        gate_slot = sb("gate_slot", [P, NBLK], F32)
        slot_token = sb("slot_token", [P, NBLK], U32)
        blk_expert = sb("blk_expert", [P, NBLK], I32)
        blk_parity = sb("blk_parity", [P, 2, NBLK], F32)

        with ExitStack() as a:
            ctx_in = sb("ctx_in", [P, 4, D], F32, a)
            xn = sb("xn", [P, D], F32, a)
            xn_t = sb("xn_t", [P, KD, P], F32, a)
            ctx_t = sb("ctx_t", [P, KD, P], F32, a)
            mask_words = sb("mask_words", [P, B, P // 4], I32, a)
            bias = sb("bias", [P, 2, P], F32, a)
            scores = sb("scores", [P, P], F32, a)
            probs = sb("probs", [P, P], F32, a)
            probs_t = sb("probs_t", [P, P], F32, a)
            xn2 = sb("xn2", [P, 2, D], F32, a)
            xn2_t = sb("xn2_t", [P, KD, P], F32, a)
            router_w = sb("router_w", [P, KD, E], F32, a)
            w_stage = sb("w_stage", [P, 2, WCH], F32, a)
            bn_a = sb("bn_a", [P, 6], F32, a)
            bn_b = sb("bn_b", [P, 6], F32, a)
            mv1 = sb("mv1", [P, 2, 2], F32, a)
            mv2 = sb("mv2", [P, 2, 2], F32, a)
            var1 = sb("var1", [P, 1], F32, a)
            var2 = sb("var2", [P, 1], F32, a)
            rstd1 = sb("rstd1", [P, 1], F32, a)
            rstd2 = sb("rstd2", [P, 1], F32, a)
            top = sb("top", [P, 1], F32, a)
            neg_top = sb("neg_top", [P, 1], F32, a)
            psum_p = sb("psum_p", [P, 1], F32, a)
            inv_p = sb("inv_p", [P, 1], F32, a)
            factor = sb("factor", [P, 2, 1], F32, a)
        mask_u8 = mask_words[:, :, :].bitcast(mybir.dt.uint8)
        with ExitStack() as b:
            rs = sb("rs", [P, B, E], F32, b)
            rs2 = sb("rs2", [P, B, E], F32, b)
            not_top = sb("not_top", [P, B, E], F32, b)
            cand = sb("cand", [P, B, E], F32, b)
            top1 = sb("top1", [P, B], F32, b)
            top2 = sb("top2", [P, B], F32, b)
            first1 = sb("first1", [P, B], F32, b)
            first2 = sb("first2", [P, B], F32, b)
            hot1 = sb("hot1", [P, B, E], F32, b)
            hot2 = sb("hot2", [P, B, E], F32, b)
            hot16 = sb("hot16", [P, B, E], F16, b)
            exp_d = sb("exp_d", [P, B], F32, b)
            gap = sb("gap", [P, B], F32, b)
            denom = sb("denom", [P, B], F32, b)
            totals = sb("totals", [P, P], F16, b)
            blocks_i = sb("blocks_i", [P, 2, E], I32, b)
            blocks_f = sb("blocks_f", [P, E], F32, b)
            start_terms = sb("start_terms", [P, E, E], F32, b)
            start = sb("start", [P, E], F32, b)
            slot = sb("slot", [P, B, E], F32, b)
            picked = sb("picked", [P, 2, B, E], F32, b)
            slot_f = sb("slot_f", [P, NA], F32, b)
            slot_i = sb("slot_i", [P, 3, NA], I32, b)
            slot_hl = sb("slot_hl", [P, 2, NA], F32, b)
            begun = sb("begun", [P, NBLK, E - 1], F16, b)
            blk_f = sb("blk_f", [P, NBLK], F32, b)
            blk_odd = sb("blk_odd", [P, NBLK], I32, b)
            gate = sb("gate", [P, NA], F32, b)
            token_val = sb("token_val", [P, NA], F32, b)
            hot_row = sb("hot_row", [P, NA, P], F32, b)
            hot_blk = sb("hot_blk", [P, NA, NBLK], F16, b)
            hot_val = sb("hot_val", [P, NA, 2, NBLK], F32, b)
        with ExitStack() as c:
            idx = [sb(f"idx{u}", [P, 1], U32, c) for u in range(2)]
            idx_out = [sb(f"idx_out{u}", [P, 1], U32, c) for u in range(2)]
            xg = sb("xg", [P, 2, D], F32, c)
            xg_hi = sb("xg_hi", [P, 2, KD, P], F32R, c)
            xg_lo = sb("xg_lo", [P, 2, KD, P], F32R, c)
            act_g = sb("act_g", [P, 2, F], F32, c)
            hid = sb("hid", [P, 2, 2, P], F32, c)
            hid_hi = sb("hid_hi", [P, 2, 2, P], F32R, c)
            hid_lo = sb("hid_lo", [P, 2, 2, P], F32R, c)
            y = sb("y", [P, 2, D], F32, c)

        with ExitStack() as a:
            ps_x = ps("ps_x", [P, KD, P], F32, a)
            ps_c = ps("ps_c", [P, KD, P], F32, a)
            ps_s = ps("ps_s", [P, 512], F32, a)
            ps_p = ps("ps_p", [P, 512], F32, a)
            ps_r = ps("ps_r", [P, 2, 512], F32, a)
            ps_x2 = ps("ps_x2", [P, KD, P], F32, a)
            ps_router = ps("ps_router", [P, B * E], F32, a)
        with ExitStack() as b:
            ps_total = ps("ps_total", [P, 512], F32, b)
            ps_rank = ps("ps_rank", [P, 512], F32, b)
            ps_count = ps("ps_count", [P, 512], F32, b)
            ps_inv = ps("ps_inv", [P, 512], F32, b)
        with ExitStack() as c:
            ps_xg = ps("ps_xg", [P, 2, KD, P], F32, c)
            ps_gu = ps("ps_gu", [P, 2, 512], F32, c)
            ps_h = ps("ps_h", [P, 2, 512], F32, c)
            ps_y = ps("ps_y", [P, 2, 512], F32, c)

        const_made = sem("const_made")
        same_made = sem("same_made")
        batch_made = sem("batch_made")
        mask_loaded = sem("mask_loaded")
        router_loaded = sem("router_loaded")
        xc_loaded = [sem(f"xc_loaded{u}") for u in range(4)]
        w_loaded = [sem(f"w_loaded{u}") for u in range(2)]
        w_hi_done = sem("w_hi_done")
        w_lo_done = sem("w_lo_done")
        valid_done = sem("valid_done")
        mask_copied = sem("mask_copied")
        bias_done = sem("bias_done")
        bn1_done = sem("bn1_done")
        mv1_done = sem("mv1_done")
        var1_done = sem("var1_done")
        rstd1_done = sem("rstd1_done")
        xn_done = sem("xn_done")
        x_turned = sem("x_turned")
        c_turned = sem("c_turned")
        xt_ready = sem("xt_ready")
        ct_ready = sem("ct_ready")
        scored = sem("scored")
        top_done = sem("top_done")
        neg_done = sem("neg_done")
        exp_done = sem("exp_done")
        inv_done = sem("inv_done")
        factor_done = sem("factor_done")
        p_turned = sem("p_turned")
        pt_ready = sem("pt_ready")
        read_out = sem("read_out")
        x1_done = sem("x1_done")
        x1_stored = sem("x1_stored")
        zeros_made = sem("zeros_made")
        pads_stored = sem("pads_stored")
        bn2_done = sem("bn2_done")
        mv2_done = sem("mv2_done")
        var2_done = sem("var2_done")
        rstd2_done = sem("rstd2_done")
        xn2_done = sem("xn2_done")
        xn2_stored = [sem(f"xn2_stored{u}") for u in range(2)]
        x2_turned = sem("x2_turned")
        x2t_ready = sem("x2t_ready")
        routed = sem("routed")
        sort_step = sem("sort_step")
        hot16_done = sem("hot16_done")
        totaled = sem("totaled")
        totals_done = sem("totals_done")
        ranked = sem("ranked")
        gap_done = sem("gap_done")
        exp_d_done = sem("exp_d_done")
        slot_hl_done = sem("slot_hl_done")
        hot_val_done = sem("hot_val_done")
        hot_row_done = sem("hot_row_done")
        hot_blk_done = sem("hot_blk_done")
        inverted = sem("inverted")
        slot_token_done = sem("slot_token_done")
        blk_done = sem("blk_done")
        gate_slot_done = sem("gate_slot_done")
        idx_done = sem("idx_done")
        gathered = [sem(f"gathered{u}") for u in range(2)]
        g_turned = sem("g_turned")
        g_hi = sem("g_hi")
        g_lo = sem("g_lo")
        gate_up = sem("gate_up")
        silu_done = sem("silu_done")
        hid_done = sem("hid_done")
        h_turned = sem("h_turned")
        h_hi = sem("h_hi")
        h_lo = sem("h_lo")
        down = sem("down")
        y_done = sem("y_done")
        idx_out_done = sem("idx_out_done")
        scattered = [sem(f"scattered{u}") for u in range(2)]
        waits_alone = sem("waits_alone")

        block = ctx.enter_context(nc.Block())

        def over_batches(eng, step, ahead, behind):
            rounds = (B - ahead - behind) // 4
            for i in range(-ahead, behind):
                step(0, i)
            with eng.Fori(0, rounds) as r:
                for u in range(behind, behind + 4):
                    step(r, u)
            for i in range(behind + 4 * rounds, B + behind):
                step(0, i)

        def on(r, u, shift, n=B):
            return not isinstance(r, int) or 0 <= 4 * r + u + shift < n

        def over_blocks(eng, step, ahead, behind):
            rounds = (NBLK - 4 - ahead) // 2
            for i in range(-ahead, 4):
                step(0, i)
            with eng.Fori(0, rounds) as r:
                for u in range(4, 6):
                    step(r, u)
            for i in range(4 + 2 * rounds, NBLK + behind):
                step(0, i)

        def has(r, u, shift):
            return not isinstance(r, int) or 0 <= u + shift < NBLK

        def wait_alone(eng, signal, value):
            eng.wait_ge(signal, value)
            eng.sem_inc(waits_alone, 1)

        @block.sync
        def _(sp):
            sp.dma_start(x1[:, 0, :], x[0]).then_inc(xc_loaded[0], 16)
            sp.dma_start(ctx_in[:, 0, :], ctx_tokens[0]).then_inc(xc_loaded[0], 16)
            sp.dma_start(mask_words[:, :, :], mask.partition_broadcast(P)).then_inc(mask_loaded, 16)
            for i in range(1, 4):
                sp.dma_start(x1[:, i, :], x[i]).then_inc(xc_loaded[i], 16)
                sp.dma_start(ctx_in[:, i, :], ctx_tokens[i]).then_inc(xc_loaded[i], 16)
                if i == 1:
                    sp.dma_start(router_w[:, :, :], router_t).then_inc(router_loaded, 16)
                if i <= 2:
                    sp.dma_start(w_stage[:, i - 1, :], weights[i - 1]).then_inc(w_loaded[i - 1], 16)

            sp.wait_ge(zeros_made, 1)
            sp.dma_start(xn2_rows[T:T + P, :], xn2[:, 1, :]).then_inc(pads_stored, 16)
            sp.dma_start(out[T:T + P, :], xn2[:, 1, :]).then_inc(pads_stored, 16)

            def batch(r, u):
                i = 4 * r + u
                if on(r, u, 2):
                    sp.wait_ge(w_hi_done, i + 1)
                    sp.wait_ge(w_lo_done, i + 1)
                    sp.dma_start(w_stage[:, u % 2, :], weights[i + 2]).then_inc(w_loaded[u % 2], 16)
                if on(r, u, -1):
                    sp.wait_ge(xn2_done, i)
                    sp.dma_start(xn2_rows[bass.ds((i - 1) * P, P), :],
                                 xn2[:, (u - 1) % 2, :]).then_inc(xn2_stored[(u - 1) % 2], 16)
                if on(r, u, 4):
                    sp.wait_ge(read_out, i + 1)
                    sp.dma_start(x1[:, i + 4, :], x[i + 4]).then_inc(xc_loaded[u % 4], 16)
                    sp.dma_start(ctx_in[:, u % 4, :], ctx_tokens[i + 4]).then_inc(xc_loaded[u % 4], 16)

            for i in range(0, 4):
                batch(0, i)
            with sp.Fori(1, B // 4 - 1) as r:
                for u in range(4):
                    batch(r, u)
            for i in range(B - 4, B + 1):
                batch(0, i)

            sp.wait_ge(x1_done, B)
            for i in range(0, B, 4):
                sp.dma_start(out[i * P:(i + 4) * P, :].rearrange("(b p) d -> p b d", p=P),
                             x1[:, i:i + 4, :]).then_inc(x1_stored, 16)
            sp.wait_ge(x1_stored, 16 * (B // 4))
            sp.wait_ge(scattered[0], 16 * ((NBLK + 1) // 2))
            sp.wait_ge(scattered[1], 16 * (NBLK // 2))

        @block.gpsimd
        def _(pool):
            g = nc.gpsimd
            g.memset(minus_half[:, :], -0.5)
            g.memset(eps_col[:, :], EPS).then_inc(const_made, 1)
            g.memset(ident[:, :], 0.0).then_inc(const_made, 1)
            pool.wait_ge(const_made, 2)
            g.affine_select(out=ident[:, :], in_=ident[:, :], compare_op=ALU.not_equal, fill=1.0, base=0,
                            pattern=[[-1, P]], channel_multiplier=1).then_inc(const_made, 1)
            g.memset(xn2[:, 1, :], 0.0).then_inc(zeros_made, 1)
            pool.wait_ge(mask_loaded, 16)

            def batch(r, u):
                i = 4 * r + u
                if on(r, u, 1):
                    if on(r, u, -1):
                        pool.wait_ge(top_done, i)
                    g.tensor_copy(bias[:, (u + 1) % 2, :], mask_u8[:, i + 1, :]).then_inc(mask_copied, 1)
                    wait_alone(pool, mask_copied, i + 2)
                    g.tensor_scalar(bias[:, (u + 1) % 2, :], bias[:, (u + 1) % 2, :], -MASKED / SCALE,
                                    MASKED / SCALE, ALU.mult, ALU.add).then_inc(bias_done, 1)
                if on(r, u, 2):
                    pool.wait_ge(mv1_done, i + 3)
                    g.tensor_tensor(var1[:, :], mv1[:, u % 2, 1:2], eps_col[:, :], ALU.add).then_inc(var1_done, 1)
                    pool.wait_ge(var1_done, i + 3)
                    if on(r, u, 1):
                        pool.wait_ge(xn_done, i + 2)
                    g.tensor_tensor(rstd1[:, :], var1[:, :], minus_half[:, :], ALU.pow).then_inc(rstd1_done, 1)
                if on(r, u, -1):
                    pool.wait_ge(mv2_done, i)
                    g.tensor_tensor(var2[:, :], mv2[:, (u - 1) % 2, 1:2], eps_col[:, :],
                                    ALU.add).then_inc(var2_done, 1)
                    pool.wait_ge(var2_done, i)
                    if on(r, u, -2):
                        pool.wait_ge(xn2_done, i - 1)
                    g.tensor_tensor(rstd2[:, :], var2[:, :], minus_half[:, :], ALU.pow).then_inc(rstd2_done, 1)
                if on(r, u, 0):
                    pool.wait_ge(w_hi_done, i + 1)
                    g.tensor_tensor(w_lo[:, bass.ds(i * WCH, WCH)], w_stage[:, u % 2, :],
                                    w_hi[:, bass.ds(i * WCH, WCH)].bitcast(F32),
                                    ALU.subtract).then_inc(w_lo_done, 1)
                if isinstance(r, int) and u == 0:
                    sort_constants()

            def sort_constants():
                g.memset(ones16[:, :], 1.0).then_inc(const_made, 1)
                g.iota(row_iota[:, :], [[1, P]], base=0, channel_multiplier=0,
                       allow_small_or_imprecise_dtypes=True).then_inc(const_made, 1)
                g.iota(blk_iota[:, :], [[1, NBLK]], base=0, channel_multiplier=0,
                       allow_small_or_imprecise_dtypes=True).then_inc(const_made, 1)
                g.iota(token_off[:, :, :], [[0, TOP_K], [P, B]], base=-T, channel_multiplier=1,
                       allow_small_or_imprecise_dtypes=True).then_inc(const_made, 1)
                g.iota(pad_token[:, :], [[0, 1]], base=T, channel_multiplier=1,
                       allow_small_or_imprecise_dtypes=True).then_inc(const_made, 1)
                g.iota(expert_iota[:, :, :], [[0, B], [1, E]], base=0, channel_multiplier=0,
                       allow_small_or_imprecise_dtypes=True).then_inc(const_made, 1)
                g.memset(before_expert[:, :, :], 1.0).then_inc(const_made, 1)
                pool.wait_ge(const_made, 10)
                g.affine_select(out=before_expert[:, :, :], in_=before_expert[:, :, :], compare_op=ALU.is_gt,
                                fill=0.0, base=0, pattern=[[1, E], [-1, E]],
                                channel_multiplier=0).then_inc(const_made, 1)
                g.affine_select(out=before_token[:, :], in_=ones16[:, :], compare_op=ALU.is_gt,
                                fill=0.0, base=0, pattern=[[1, P]],
                                channel_multiplier=-1).then_inc(const_made, 1)
                pool.wait_ge(batch_made, 1)
                g.affine_select(out=before_batch[:, :, :], in_=before_batch[:, :, :], compare_op=ALU.is_gt,
                                fill=0.0, base=0, pattern=[[E, B], [0, E]],
                                channel_multiplier=-1).then_inc(batch_made, 1)

            over_batches(pool, batch, 2, 2)

            pool.wait_ge(hot_blk_done, 1)
            for first in range(0, NA, NA // 2):
                n = slice(first, first + NA // 2)
                for k, value in enumerate((token_val, gate)):
                    g.tensor_tensor(hot_val[:, n, k, :], hot_blk[:, n, :],
                                    value[:, n].unsqueeze(2).to_broadcast([P, NA // 2, NBLK]),
                                    ALU.mult).then_inc(hot_val_done, 1)

            pool.wait_ge(slot_token_done, 1)
            pool.wait_ge(pads_stored, 32)
            pool.wait_ge(xn2_stored[0], 16 * (B // 2))
            pool.wait_ge(xn2_stored[1], 16 * (B // 2))

            def blocks(r, u):
                b = 2 * r + u
                if has(r, u, 3):
                    v = u + 3
                    if has(r, u, 1):
                        pool.wait_ge(gathered[v % 2], 16 * r + 16 * ((v - 2) // 2 + 1))
                        pool.wait_ge(g_turned, b + 2)
                    g.tensor_copy(idx[v % 2][:, :], slot_token[:, bass.ds(b + 3, 1)]).then_inc(idx_done, 1)
                    wait_alone(pool, idx_done, b + 4)
                    g.indirect_dma_start(out=xg[:, v % 2, :], out_offset=None, in_=xn2_rows[:, :],
                                         in_offset=bass.IndirectOffsetOnAxis(ap=idx[v % 2][:, 0:1], axis=0)
                                         ).then_inc(gathered[v % 2], 16)
                if has(r, u, -3):
                    v = u - 3
                    if has(r, u, -4):
                        pool.wait_ge(scattered[(v - 1) % 2], 16 * r + 16 * ((v - 1) // 2 + 1))
                    else:
                        pool.wait_ge(x1_stored, 16 * (B // 4))
                    g.tensor_copy(idx_out[v % 2][:, :], slot_token[:, bass.ds(b - 3, 1)]).then_inc(idx_out_done, 1)
                    pool.wait_ge(idx_out_done, b - 2)
                    wait_alone(pool, y_done, b - 2)
                    g.indirect_dma_start(out=out[:, :],
                                         out_offset=bass.IndirectOffsetOnAxis(ap=idx_out[v % 2][:, 0:1], axis=0),
                                         in_=y[:, v % 2, :], in_offset=None,
                                         compute_op=ALU.add).then_inc(scattered[v % 2], 16)

            over_blocks(pool, blocks, 3, 3)

        @block.tensor
        def _(pe):
            t = nc.tensor
            pe.wait_ge(const_made, 3)
            pe.wait_ge(router_loaded, 16)

            def batch(r, u):
                i = 4 * r + u
                if on(r, u, 0):
                    pe.wait_ge(xt_ready, i + 1)
                    pe.wait_ge(ct_ready, i + 1)
                    if on(r, u, -1):
                        pe.wait_ge(top_done, i)
                    for k in range(KD):
                        mm = t.matmul(ps_s[:, 0:P], xn_t[:, k, :], ctx_t[:, k, :],
                                      start=(k == 0), stop=(k == KD - 1))
                    mm.then_inc(scored, 1)
                if on(r, u, 1):
                    v = u + 1
                    pe.wait_ge(xc_loaded[v % 4], 32 * r + 32 * (v // 4 + 1))
                    if on(r, u, 0):
                        pe.wait_ge(ct_ready, i + 1)
                    for k in range(KD):
                        mm = t.transpose(ps_c[:, k, :], ctx_in[:, v % 4, k * P:(k + 1) * P], ident[:, :])
                    mm.then_inc(c_turned, 1)
                    pe.wait_ge(xn_done, i + 2)
                    for k in range(KD):
                        mm = t.transpose(ps_x[:, k, :], xn[:, k * P:(k + 1) * P], ident[:, :])
                    mm.then_inc(x_turned, 1)
                if on(r, u, -3):
                    pe.wait_ge(x2t_ready, i - 2)
                    for k in range(KD):
                        mm = t.matmul(ps_router[:, bass.ds((i - 3) * E, E)], xn2_t[:, k, :], router_w[:, k, :],
                                      start=(k == 0), stop=(k == KD - 1))
                    mm.then_inc(routed, 1)
                if on(r, u, 0):
                    pe.wait_ge(exp_done, i + 1)
                    t.transpose(ps_p[:, 0:P], probs[:, :], ident[:, :]).then_inc(p_turned, 1)
                if on(r, u, -2):
                    pe.wait_ge(xn2_done, i - 1)
                    for k in range(KD):
                        mm = t.transpose(ps_x2[:, k, :], xn2[:, u % 2, k * P:(k + 1) * P], ident[:, :])
                    mm.then_inc(x2_turned, 1)
                if on(r, u, 0):
                    pe.wait_ge(pt_ready, i + 1)
                    if on(r, u, -2):
                        pe.wait_ge(x1_done, i - 1)
                    t.matmul(ps_r[:, u % 2, :], probs_t[:, :], ctx_in[:, u % 4, :],
                             start=True, stop=True).then_inc(read_out, 1)

            over_batches(pe, batch, 1, 3)

            pe.wait_ge(hot16_done, 1)
            t.matmul(ps_total[:, 0:1], hot16.rearrange("p b e -> p (b e)"), ones16[:, 0:1],
                     start=True, stop=True).then_inc(totaled, 1)
            pe.wait_ge(totals_done, 1)
            pe.wait_ge(batch_made, 2)
            t.matmul(ps_count[:, 0:E], totals[:, :], same_expert[:, :], start=True, stop=True).then_inc(ranked, 1)
            pe.wait_ge(const_made, 12)
            t.matmul(ps_rank[:, 0:P], before_token[:, :], hot16.rearrange("p b e -> p (b e)"),
                     start=True, stop=False)
            t.matmul(ps_rank[:, 0:P], totals[:, :], before_batch.rearrange("p b e -> p (b e)"),
                     start=False, stop=True).then_inc(ranked, 1)
            for n in range(NA):
                if n % CHUNK == 0:
                    pe.wait_ge(hot_row_done, n // CHUNK + 1)
                if n % (NA // 2) == 0:
                    pe.wait_ge(hot_val_done, 2 * (n // (NA // 2)) + 2)
                mm = t.matmul(ps_inv[:, 0:2 * NBLK], hot_row[:, n, :], hot_val[:, n, :, :],
                              start=(n == 0), stop=(n == NA - 1))
            mm.then_inc(inverted, 1)

            pe.wait_ge(w_hi_done, B)
            pe.wait_ge(w_lo_done, B)
            pe.wait_ge(blk_done, 1)
            pe.wait_ge(slot_token_done, 1)

            def expert_of(b):
                return pe.value_load(blk_expert[0:1, bass.ds(b, 1)], min_val=0, max_val=E - 1)

            def blocks(r, u):
                b = 2 * r + u
                if has(r, u, 0):
                    e = expert_of(b)
                if has(r, u, -2):
                    e_down = expert_of(b - 2)
                if has(r, u, 0):
                    pe.wait_ge(g_hi, b + 1)
                    pe.wait_ge(g_lo, b + 1)
                    if has(r, u, -2):
                        pe.wait_ge(hid_done, b - 1)
                    n = 0
                    for k in range(KD):
                        for lhs, w in ((xg_hi, w_hi), (xg_hi, w_lo), (xg_lo, w_hi)):
                            mm = t.matmul(ps_gu[:, u % 2, 0:2 * F], lhs[:, u % 2, k, :],
                                          w[:, bass.ds(e * WGU + k * 2 * F, 2 * F)],
                                          start=(n == 0), stop=(n == 3 * KD - 1))
                            n += 1
                    mm.then_inc(gate_up, 1)
                if has(r, u, 2):
                    v = u + 2
                    pe.wait_ge(gathered[v % 2], 16 * r + 16 * (v // 2 + 1))
                    if has(r, u, 0):
                        pe.wait_ge(g_lo, b + 1)
                        pe.wait_ge(g_hi, b + 1)
                    for k in range(KD):
                        mm = t.transpose(ps_xg[:, v % 2, k, :], xg[:, v % 2, k * P:(k + 1) * P], ident[:, :])
                    mm.then_inc(g_turned, 1)
                if has(r, u, -1):
                    v = u - 1
                    pe.wait_ge(hid_done, b)
                    if has(r, u, -3):
                        pe.wait_ge(h_hi, b - 2)
                        pe.wait_ge(h_lo, b - 2)
                    for half in range(2):
                        mm = t.transpose(ps_h[:, v % 2, half * P:(half + 1) * P], hid[:, v % 2, half, :], ident[:, :])
                    mm.then_inc(h_turned, 1)
                if has(r, u, -2):
                    pe.wait_ge(h_hi, b - 1)
                    pe.wait_ge(h_lo, b - 1)
                    if has(r, u, -4):
                        pe.wait_ge(y_done, b - 3)
                    n = 0
                    for half, base, row in ((0, WA0, e_down), (1, WB0, e_down // 2)):
                        for lhs, w in ((hid_hi, w_hi), (hid_hi, w_lo), (hid_lo, w_hi)):
                            mm = t.matmul(ps_y[:, u % 2, :], lhs[:, u % 2, half, :],
                                          w[:, bass.ds(row * D + base, D)],
                                          start=(n == 0), stop=(n == 5))
                            n += 1
                    mm.then_inc(down, 1)

            over_blocks(pe, blocks, 2, 2)

        @block.scalar
        def _(act):
            s = nc.scalar

            def batch(r, u):
                i = 4 * r + u
                if on(r, u, 0):
                    pe_free = on(r, u, -1)
                    act.wait_ge(neg_done, i + 1)
                    if pe_free:
                        act.wait_ge(p_turned, i)
                    s.activation(probs[:, :], scores[:, :], ACT.Exp, bias=neg_top[:, :],
                                 accum_out=psum_p[:, :]).then_inc(exp_done, 1)
                if on(r, u, 1):
                    act.wait_ge(c_turned, i + 2)
                    if on(r, u, 0):
                        act.wait_ge(scored, i + 1)
                    s.activation(ctx_t[:, :, :], ps_c[:, :, :], ACT.Copy).then_inc(ct_ready, 1)
                    act.wait_ge(x_turned, i + 2)
                    s.activation(xn_t[:, :, :], ps_x[:, :, :], ACT.Copy).then_inc(xt_ready, 1)
                if on(r, u, 0):
                    act.wait_ge(p_turned, i + 1)
                    if on(r, u, -1):
                        act.wait_ge(read_out, i)
                    s.activation(probs_t[:, :], ps_p[:, 0:P], ACT.Copy).then_inc(pt_ready, 1)
                if on(r, u, -2):
                    act.wait_ge(x2_turned, i - 1)
                    if on(r, u, -3):
                        act.wait_ge(routed, i - 2)
                    s.activation(xn2_t[:, :, :], ps_x2[:, :, :], ACT.Copy).then_inc(x2t_ready, 1)
                if on(r, u, 0):
                    act.wait_ge(w_loaded[u % 2], 32 * r + 16 * (u // 2 + 1))
                    s.activation(w_hi[:, bass.ds(i * WCH, WCH)], w_stage[:, u % 2, :],
                                 ACT.Copy).then_inc(w_hi_done, 1)

            over_batches(act, batch, 1, 3)

            act.wait_ge(gap_done, 1)
            s.activation(exp_d[:, :], gap[:, :], ACT.Exp).then_inc(exp_d_done, 1)
            act.wait_ge(gate_slot_done, 1)

            def blocks(r, u):
                b = 2 * r + u
                if has(r, u, 0):
                    act.wait_ge(gate_up, b + 1)
                    if has(r, u, -2):
                        act.wait_ge(hid_done, b - 1)
                    s.activation(act_g[:, u % 2, :], ps_gu[:, u % 2, 0:F], ACT.Silu).then_inc(silu_done, 1)
                if has(r, u, 2):
                    v = u + 2
                    act.wait_ge(g_turned, b + 3)
                    if has(r, u, 0):
                        act.wait_ge(gate_up, b + 1)
                    s.activation(xg_hi[:, v % 2, :, :], ps_xg[:, v % 2, :, :], ACT.Copy).then_inc(g_hi, 1)
                if has(r, u, -1):
                    v = u - 1
                    act.wait_ge(h_turned, b)
                    if has(r, u, -3):
                        act.wait_ge(down, b - 2)
                    s.activation(hid_hi[:, v % 2, :, :], ps_h[:, v % 2, 0:2 * P],
                                 ACT.Copy).then_inc(h_hi, 1)
                if has(r, u, -2):
                    act.wait_ge(down, b - 1)
                    if has(r, u, -4):
                        act.wait_ge(scattered[u % 2], 16 * r + 16 * ((u - 4) // 2 + 1))
                    s.activation(y[:, u % 2, :], ps_y[:, u % 2, :], ACT.Copy,
                                 scale=gate_slot[:, bass.ds(b - 2, 1)]).then_inc(y_done, 1)

            over_blocks(act, blocks, 2, 2)

        @block.vector
        def _(dve):
            v_ = nc.vector
            dve.wait_ge(const_made, 3)
            with nc.allow_low_precision("zeros and ones"):
                v_.tensor_reduce(same_expert[:, :], ident.rearrange("p (b e) -> p e b", e=E), AX.X,
                                 ALU.add).then_inc(same_made, 1)
            dve.wait_ge(same_made, 1)
            v_.tensor_copy(before_batch[:, :, :],
                           same_expert[:, :].unsqueeze(1).to_broadcast([P, B, E])).then_inc(batch_made, 1)

            def batch(r, u):
                i = 4 * r + u
                if on(r, u, 0):
                    if on(r, u, -1):
                        dve.wait_ge(exp_done, i)
                    dve.wait_ge(bias_done, i + 1)
                    wait_alone(dve, scored, i + 1)
                    v_.tensor_tensor_reduce(scores[:, :], ps_s[:, 0:P], bias[:, u % 2, :], SCALE, LOWEST,
                                            ALU.add, ALU.max, top[:, :]).then_inc(top_done, 1)
                    dve.wait_ge(top_done, i + 1)
                    v_.tensor_scalar(neg_top[:, :], top[:, :], -1.0, None, ALU.mult).then_inc(neg_done, 1)
                if on(r, u, -1):
                    v = u - 1
                    dve.wait_ge(read_out, i)
                    dve.wait_ge(factor_done, i)
                    v_.scalar_tensor_tensor(x1[:, i - 1, :], ps_r[:, v % 2, :], factor[:, v % 2, :],
                                            x1[:, i - 1, :], ALU.mult, ALU.add).then_inc(x1_done, 1)
                    wait_alone(dve, x1_done, i)
                    v_.bn_stats(bn_b[:, :], x1[:, i - 1, :]).then_inc(bn2_done, 1)
                    wait_alone(dve, bn2_done, i)
                    v_.bn_aggr(mv2[:, v % 2, :], bn_b[:, :]).then_inc(mv2_done, 1)
                if on(r, u, 0):
                    dve.wait_ge(exp_done, i + 1)
                    v_.reciprocal(inv_p[:, :], psum_p[:, :]).then_inc(inv_done, 1)
                    dve.wait_ge(inv_done, i + 1)
                    if isinstance(r, int) and u == 0:
                        dve.wait_ge(valid_done, 1)
                    v_.tensor_scalar(factor[:, u % 2, :], inv_p[:, :], valid[:, bass.ds(i, 1)], None,
                                     ALU.mult).then_inc(factor_done, 1)
                if on(r, u, 2):
                    dve.wait_ge(rstd1_done, i + 3)
                    if on(r, u, 1):
                        dve.wait_ge(x_turned, i + 2)
                    v_.tensor_scalar(xn[:, :], x1[:, i + 2, :], mv1[:, u % 2, 0:1], rstd1[:, :],
                                     ALU.subtract, ALU.mult).then_inc(xn_done, 1)
                if on(r, u, 3):
                    v = u + 3
                    wait_alone(dve, xc_loaded[v % 4], 32 * r + 32 * (v // 4 + 1))
                    v_.bn_stats(bn_a[:, :], x1[:, i + 3, :]).then_inc(bn1_done, 1)
                    wait_alone(dve, bn1_done, i + 4)
                    v_.bn_aggr(mv1[:, v % 2, :], bn_a[:, :]).then_inc(mv1_done, 1)
                if isinstance(r, int) and u == -1:
                    dve.wait_ge(mask_loaded, 16)
                    v_.tensor_reduce(valid[:, :], mask_u8, AX.X, ALU.max).then_inc(valid_done, 1)
                if on(r, u, -1):
                    dve.wait_ge(rstd2_done, i)
                    if isinstance(r, int) and u == 2:
                        dve.wait_ge(pads_stored, 32)
                    if on(r, u, -3):
                        dve.wait_ge(x2_turned, i - 2)
                        dve.wait_ge(xn2_stored[(u - 1) % 2], 32 * r + 16 * ((u - 3) // 2 + 1))
                    v_.tensor_scalar(xn2[:, (u - 1) % 2, :], x1[:, i - 1, :], mv2[:, (u - 1) % 2, 0:1],
                                     rstd2[:, :], ALU.subtract, ALU.mult).then_inc(xn2_done, 1)

            over_batches(dve, batch, 3, 3)

            chain = [0]

            def then(ins):
                chain[0] += 1
                ins.then_inc(sort_step, 1)
                dve.wait_ge(sort_step, chain[0])

            def over_e(m):
                return m.unsqueeze(2).to_broadcast([P, B, E])

            dve.wait_ge(routed, B)
            dve.wait_ge(xn2_stored[0], 16 * (B // 2))
            dve.wait_ge(xn2_stored[1], 16 * (B // 2))
            dve.wait_ge(const_made, 12)
            dve.wait_ge(batch_made, 2)
            then(v_.tensor_copy(rs[:, :, :], ps_router.rearrange("p (b e) -> p b e", e=E)))
            then(v_.tensor_reduce(top1[:, :], rs[:, :, :], AX.X, ALU.max))
            then(v_.tensor_tensor(not_top[:, :, :], rs[:, :, :], over_e(top1[:, :]), ALU.is_lt))
            then(v_.scalar_tensor_tensor(cand[:, :, :], not_top[:, :, :], float(E), expert_iota[:, :, :],
                                         ALU.mult, ALU.add))
            then(v_.tensor_reduce(first1[:, :], cand[:, :, :], AX.X, ALU.min))
            then(v_.tensor_tensor(hot1[:, :, :], expert_iota[:, :, :], over_e(first1[:, :]), ALU.is_equal))
            then(v_.scalar_tensor_tensor(rs2[:, :, :], hot1[:, :, :], LOWEST, rs[:, :, :], ALU.mult, ALU.add))
            then(v_.tensor_reduce(top2[:, :], rs2[:, :, :], AX.X, ALU.max))
            then(v_.tensor_tensor(not_top[:, :, :], rs2[:, :, :], over_e(top2[:, :]), ALU.is_lt))
            then(v_.scalar_tensor_tensor(cand[:, :, :], not_top[:, :, :], float(E), expert_iota[:, :, :],
                                         ALU.mult, ALU.add))
            then(v_.tensor_reduce(first2[:, :], cand[:, :, :], AX.X, ALU.min))
            then(v_.tensor_tensor(hot2[:, :, :], expert_iota[:, :, :], over_e(first2[:, :]), ALU.is_equal))
            v_.tensor_tensor(hot16[:, :, :], hot1[:, :, :], hot2[:, :, :], ALU.add).then_inc(hot16_done, 1)
            v_.tensor_tensor(gap[:, :], top2[:, :], top1[:, :], ALU.subtract).then_inc(gap_done, 1)
            dve.wait_ge(totaled, 1)
            v_.tensor_scalar(totals[:, :], ones16[:, :], ps_total[:, 0:1], None, ALU.mult).then_inc(totals_done, 1)
            dve.wait_ge(exp_d_done, 1)
            then(v_.tensor_scalar(denom[:, :], exp_d[:, :], 1.0, None, ALU.add))
            then(v_.reciprocal(gate[:, 0:B], denom[:, :]))
            then(v_.tensor_tensor(gate[:, B:NA], gate[:, 0:B], exp_d[:, :], ALU.mult))
            dve.wait_ge(ranked, 1)
            then(v_.tensor_scalar(blocks_i[:, 0, :], ps_count[:, 0:E], float(P - 1), None, ALU.add))
            then(v_.tensor_scalar(blocks_i[:, 1, :], blocks_i[:, 0, :], 7, None, ALU.logical_shift_right))
            then(v_.tensor_copy(blocks_f[:, :], blocks_i[:, 1, :]))
            then(v_.tensor_tensor(start_terms[:, :, :], before_expert[:, :, :],
                                  blocks_f[:, :].unsqueeze(1).to_broadcast([P, E, E]), ALU.mult))
            then(v_.tensor_reduce(start[:, :], start_terms[:, :, :], AX.X, ALU.add))
            dve.wait_ge(ranked, 2)
            then(v_.scalar_tensor_tensor(slot[:, :, :], start[:, :].unsqueeze(1).to_broadcast([P, B, E]), float(P),
                                         ps_rank[:, 0:P].rearrange("p (b e) -> p b e", e=E),
                                         ALU.mult, ALU.add))
            v_.tensor_tensor(picked[:, 0, :, :], hot1[:, :, :], slot[:, :, :], ALU.mult)
            then(v_.tensor_tensor(picked[:, 1, :, :], hot2[:, :, :], slot[:, :, :], ALU.mult))
            then(v_.tensor_reduce(slot_f[:, :], picked.rearrange("p k b e -> p (k b) e"), AX.X, ALU.add))
            then(v_.tensor_copy(slot_i[:, 0, :], slot_f[:, :]))
            v_.tensor_scalar(slot_i[:, 1, :], slot_i[:, 0, :], 7, None, ALU.logical_shift_right)
            then(v_.tensor_scalar(slot_i[:, 2, :], slot_i[:, 0, :], P - 1, None, ALU.bitwise_and))
            v_.tensor_copy(slot_hl[:, :, :], slot_i[:, 1:3, :]).then_inc(slot_hl_done, 1)
            dve.wait_ge(slot_hl_done, 1)
            def hot_rows(first):
                n = slice(first, first + CHUNK)
                v_.tensor_tensor(hot_row[:, n, :], row_iota[:, :].unsqueeze(1).to_broadcast([P, CHUNK, P]),
                                 slot_hl[:, 1, n].unsqueeze(2).to_broadcast([P, CHUNK, P]),
                                 ALU.is_equal).then_inc(hot_row_done, 1)

            then(v_.tensor_tensor(token_val[:, :], token_off.rearrange("p k b -> p (k b)"), slot_hl[:, 1, :],
                                  ALU.subtract))
            v_.tensor_tensor(hot_blk[:, :, :], blk_iota[:, :].unsqueeze(1).to_broadcast([P, NA, NBLK]),
                             slot_hl[:, 0, :].unsqueeze(2).to_broadcast([P, NA, NBLK]),
                             ALU.is_equal).then_inc(hot_blk_done, 1)
            for n in range(0, NA, CHUNK):
                hot_rows(n)
            then(v_.tensor_tensor(begun[:, :, :], blk_iota[:, :].unsqueeze(2).to_broadcast([P, NBLK, E - 1]),
                                  start[:, 1:E].unsqueeze(1).to_broadcast([P, NBLK, E - 1]), ALU.is_ge))
            then(v_.tensor_reduce(blk_f[:, :], begun[:, :, :], AX.X, ALU.add))
            then(v_.tensor_copy(blk_expert[:, :], blk_f[:, :]))
            then(v_.tensor_scalar(blk_odd[:, :], blk_expert[:, :], 1, None, ALU.bitwise_and))
            then(v_.tensor_copy(blk_parity[:, 1, :], blk_odd[:, :]))
            v_.tensor_scalar(blk_parity[:, 0, :], blk_parity[:, 1, :], -1.0, 1.0, ALU.mult,
                             ALU.add).then_inc(blk_done, 1)
            dve.wait_ge(blk_done, 1)
            dve.wait_ge(inverted, 1)
            v_.tensor_scalar(slot_token[:, :], ps_inv[:, 0:NBLK], pad_token[:, :], None,
                             ALU.add).then_inc(slot_token_done, 1)
            v_.tensor_copy(gate_slot[:, :], ps_inv[:, NBLK:2 * NBLK]).then_inc(gate_slot_done, 1)

            def blocks(r, u):
                b = 2 * r + u
                if has(r, u, 0):
                    dve.wait_ge(silu_done, b + 1)
                    if has(r, u, -2):
                        dve.wait_ge(h_turned, b - 1)
                    v_.tensor_tensor(hid[:, u % 2, 0, :], act_g[:, u % 2, 0:P], ps_gu[:, u % 2, F:F + P],
                                     ALU.mult)
                    for odd in range(2):
                        last = v_.scalar_tensor_tensor(
                            hid[:, u % 2, 1, odd * FB:(odd + 1) * FB], act_g[:, u % 2, P:F],
                            blk_parity[:, odd, bass.ds(b, 1)], ps_gu[:, u % 2, F + P:2 * F],
                            ALU.mult, ALU.mult)
                    last.then_inc(hid_done, 1)
                if has(r, u, 2):
                    v = u + 2
                    dve.wait_ge(g_hi, b + 3)
                    v_.tensor_tensor(xg_lo[:, v % 2, :, :], ps_xg[:, v % 2, :, :],
                                     xg_hi[:, v % 2, :, :].bitcast(F32), ALU.subtract).then_inc(g_lo, 1)
                if has(r, u, -1):
                    v = u - 1
                    dve.wait_ge(h_hi, b)
                    v_.tensor_tensor(hid_lo[:, v % 2, :, :],
                                     ps_h[:, v % 2, 0:2 * P].rearrange("p (h t) -> p h t", h=2),
                                     hid_hi[:, v % 2, :, :].bitcast(F32), ALU.subtract).then_inc(h_lo, 1)

            over_blocks(dve, blocks, 2, 1)


def kernel(x, ctx_2048, mask_BxS2_bk0, L0_ffn_w_gate_router, L0_ffn_w_gate_proj, L0_ffn_w_up_proj,
           L0_ffn_w_down_proj):
    import numpy as np
    import concourse.bacc as bacc
    from concourse import mybir as mb
    from concourse.bass_utils import run_bass_kernel_spmd

    P = 128
    x, ctx_2048 = np.asarray(x), np.asarray(ctx_2048)
    router, gate, up, down = (np.asarray(a) for a in (L0_ffn_w_gate_router, L0_ffn_w_gate_proj,
                                                      L0_ffn_w_up_proj, L0_ffn_w_down_proj))
    B, S, D = x.shape
    E, F, _ = gate.shape
    KD = D // P
    gu = np.concatenate([gate.transpose(0, 2, 1), up.transpose(0, 2, 1)], axis=2)
    gu = gu.reshape(E, KD, P, 2 * F).transpose(2, 0, 1, 3).reshape(P, -1)
    dn = down.transpose(0, 2, 1)
    first = dn[:, :P].transpose(1, 0, 2).reshape(P, -1)
    rest = dn[:, P:].reshape(E // 2, 2, F - P, D).transpose(1, 2, 0, 3).reshape(P, -1)
    w = np.concatenate([gu, first, rest], axis=1)
    w = w.reshape(P, B, -1).transpose(1, 0, 2)
    arrays = {
        "x": x,
        "ctx": ctx_2048,
        "mask": np.ascontiguousarray(mask_BxS2_bk0).view(np.int32),
        "router_t": router.transpose(1, 0).reshape(KD, P, E).transpose(1, 0, 2),
        "weights": w,
    }
    arrays = {k: np.ascontiguousarray(v) for k, v in arrays.items()}
    nc = bacc.Bacc("TRN2", target_bir_lowering=False, num_devices=1, dynamic_dma_scratch_size=8192)
    args = [nc.dram_tensor(k, v.shape, mb.dt.from_np(v.dtype), kind="ExternalInput").ap()
            for k, v in arrays.items()]
    out = nc.dram_tensor("out", (B * S + P, D), mb.dt.float32, kind="ExternalOutput").ap()
    xattn_moe_kernel(nc, *args, out)
    got = run_bass_kernel_spmd(nc, [arrays], core_ids=[0])
    return got.results[0]["out"][:B * S].reshape(B, S, D)
```

```python
from contextlib import ExitStack

import concourse.bass as bass
from concourse import mybir

ALU = mybir.AluOpType
ACT = mybir.ActivationFunctionType
AX = mybir.AxisListType
F32 = mybir.dt.float32
F32R = mybir.dt.float32r
F16 = mybir.dt.float16
BF16 = mybir.dt.bfloat16
I32 = mybir.dt.int32
U32 = mybir.dt.uint32

P = 128
EPS = 1e-5
TOP_K = 2
MASKED = -1e30
LOWEST = -3e38


def xattn_moe_kernel(nc, x, ctx_tokens, mask, router_t, weights, rest_weights, out):
    B, S, D = x.shape
    E = router_t.shape[2]
    KD = D // P
    F = rest_weights.shape[1] + P
    FB = F - P
    T = B * S
    NBLK = (TOP_K * T + E * (P - 1)) // P
    NA = TOP_K * B
    WGU = KD * 2 * F
    WDOWN = E * WGU
    WCH = (WDOWN + E * D) // B
    WHALF = WCH // 2
    WREST = E * D // B
    SCALE = float(D) ** -0.5
    STEPS = 8
    EARLY = 13
    VALUES = 5
    assert S == P and FB == P // 2 and E * B == P and WCH == weights.shape[2] and WREST == rest_weights.shape[2]

    xn2_rows = nc.dram_tensor("xn2_rows", (T + P, D), F32).ap()

    with ExitStack() as ctx:
        def sem(name):
            return ctx.enter_context(nc.semaphore(name))

        def sb(name, shape, dt, scope=ctx):
            return scope.enter_context(nc.sbuf_tensor(name, shape, dt))

        def ps(name, shape, dt, scope=ctx):
            return scope.enter_context(nc.psum_tensor(name, shape, dt))

        w_hi = sb("w_hi", [P, WDOWN + E * D], F32R)
        w_lo = sb("w_lo", [P, WDOWN + E * D], F32R)
        w_rest = sb("w_rest", [P, E * D], F32R)
        x1 = sb("x1", [P, B, D], F32)
        ident = sb("ident", [P, P], F32)
        row_iota = sb("row_iota", [P, P], BF16)
        blk_iota = sb("blk_iota", [P, NBLK], BF16)
        expert_iota = sb("expert_iota", [P, B, E], F32)
        batch_off = sb("batch_off", [P, TOP_K, B], BF16)
        row_id = sb("row_id", [P, 1], F32)
        pad_token = sb("pad_token", [P, 1], F32)
        before_expert = sb("before_expert", [P, E, E], F32)
        before_token = sb("before_token", [P, P], F16)
        before_batch = sb("before_batch", [P, B, E], F16)
        same_expert = sb("same_expert", [P, E], F16)
        ones16 = sb("ones16", [P, P], F16)
        minus_half = sb("minus_half", [P, 2], F32)
        eps_col = sb("eps_col", [P, 2], F32)
        silu_probe = sb("silu_probe", [P, 1], F32)
        valid = sb("valid", [P, B], F32)
        gate_slot = sb("gate_slot", [P, NBLK], F32)
        slot_token = sb("slot_token", [P, NBLK], U32)
        blk_experts = sb("blk_experts", [P, NBLK + 1], I32)

        with ExitStack() as a:
            ctx_in = sb("ctx_in", [P, 4, D], F32, a)
            xn = sb("xn", [P, D], F32, a)
            xn_t = sb("xn_t", [P, KD, P], F32, a)
            ctx_t = sb("ctx_t", [P, KD, P], F32, a)
            mask_words = sb("mask_words", [P, B, P // 4], I32, a)
            bias = sb("bias", [P, B, P], BF16, a)
            bias_now = sb("bias_now", [P, 2, P], BF16, a)
            scores = sb("scores", [P, P], F32, a)
            probs = sb("probs", [P, P], F32, a)
            probs_t = sb("probs_t", [P, P], F32, a)
            xn2 = sb("xn2", [P, 2, D], F32, a)
            xn2_t = sb("xn2_t", [P, KD, P], F32, a)
            router_w = sb("router_w", [P, KD, E], F32, a)
            w_stage = sb("w_stage", [P, 2, WCH], F32, a)
            rest_stage = sb("rest_stage", [FB, 2, WREST], F32, a)
            bn_a = sb("bn_a", [P, 2, 6], F32, a)
            bn_b = sb("bn_b", [P, 6], F32, a)
            mv = sb("mv", [P, 2, 2, 2], F32, a)
            var = sb("var", [P, 2, 2], F32, a)
            rstd = sb("rstd", [P, 2], F32, a)
            top = sb("top", [P, 1], F32, a)
            neg_top = sb("neg_top", [P, 1], F32, a)
            psum_p = sb("psum_p", [P, 1], F32, a)
            inv_p = sb("inv_p", [P, 2, 1], F32, a)
            factor = sb("factor", [P, 2, 1], F32, a)
        mask_u8 = mask_words[:, :, :].bitcast(mybir.dt.uint8)
        with ExitStack() as b:
            rs2 = sb("rs2", [P, B, E], F32, b)
            not_top = sb("not_top", [P, B, E], F32, b)
            cand = sb("cand", [P, B, E], F32, b)
            top1 = sb("top1", [P, B], F32, b)
            top2 = sb("top2", [P, B], F32, b)
            first1 = sb("first1", [P, B], F32, b)
            first2 = sb("first2", [P, B], F32, b)
            hot1 = sb("hot1", [P, B, E], F32, b)
            hot2 = sb("hot2", [P, B, E], F32, b)
            hot16 = sb("hot16", [P, B, E], F16, b)
            exp_d = sb("exp_d", [P, B], F32, b)
            gap = sb("gap", [P, B], F32, b)
            denom = sb("denom", [P, B], F32, b)
            totals = sb("totals", [P, P], F16, b)
            blocks_i = sb("blocks_i", [P, 2, E], I32, b)
            blocks_f = sb("blocks_f", [P, E], F32, b)
            start_terms = sb("start_terms", [P, E, E], F32, b)
            start = sb("start", [P, E], F32, b)
            slot = sb("slot", [P, B, E], F32, b)
            picked = sb("picked", [P, 2, B, E], F32, b)
            slot_f = sb("slot_f", [P, NA], F32, b)
            slot_i = sb("slot_i", [P, 3, NA], I32, b)
            slot_hl = sb("slot_hl", [P, 2, NA], F32, b)
            slot_blk = sb("slot_blk", [P, NA], BF16, b)
            row_diff = sb("row_diff", [P, NA], F32, b)
            begun = sb("begun", [P, NBLK, E - 1], F16, b)
            blk_f = sb("blk_f", [P, NBLK + 2], F32, b)
            gate = sb("gate", [P, NA], F32, b)
            gate_rest = sb("gate_rest", [P, 2, NA], F32, b)
            gate_part = sb("gate_part", [P, 3, NA], BF16, b)
            row_off = sb("row_off", [P, NBLK], F32, b)
            gate_low = sb("gate_low", [P, NBLK], F32, b)
            hot_row = sb("hot_row", [P, NA, P], BF16, b)
            hot_blk = sb("hot_blk", [P, NA, NBLK], BF16, b)
            hot_val = sb("hot_val", [P, NA, VALUES, NBLK], BF16, b)
        with ExitStack() as c:
            idx = [sb(f"idx{u}", [P, 1], U32, c) for u in range(2)]
            idx_out = [sb(f"idx_out{u}", [P, 1], U32, c) for u in range(2)]
            xg = sb("xg", [P, 2, D], F32, c)
            xg_hi = sb("xg_hi", [P, 2, KD, P], F32R, c)
            xg_lo = sb("xg_lo", [P, 2, KD, P], F32R, c)
            act_g = sb("act_g", [P, 2, F], F32, c)
            hid = sb("hid", [P, 2, 2, P], F32, c)
            hid_hi = sb("hid_hi", [P, 2, 2, P], F32R, c)
            hid_lo = sb("hid_lo", [P, 2, 2, P], F32R, c)
            y = sb("y", [P, 2, D], F32, c)

        with ExitStack() as a:
            ps_x = ps("ps_x", [P, KD, P], F32, a)
            ps_c = ps("ps_c", [P, KD, P], F32, a)
            ps_s = ps("ps_s", [P, 512], F32, a)
            ps_p = ps("ps_p", [P, 512], F32, a)
            ps_r = ps("ps_r", [P, 2, 512], F32, a)
            ps_x2 = ps("ps_x2", [P, KD, P], F32, a)
            ps_router = ps("ps_router", [P, B * E], F32, a)
        with ExitStack() as b:
            ps_total = ps("ps_total", [P, 512], F32, b)
            ps_rank = ps("ps_rank", [P, 512], F32, b)
            ps_count = ps("ps_count", [P, 512], F32, b)
            ps_inv = ps("ps_inv", [P, 512], F32, b)
        with ExitStack() as c:
            ps_xg = ps("ps_xg", [P, 2, KD, P], F32, c)
            ps_gu = ps("ps_gu", [P, 2, 512], F32, c)
            ps_h = ps("ps_h", [P, 2, 512], F32, c)
            ps_y = ps("ps_y", [P, 2, 512], F32, c)

        const_made = sem("const_made")
        same_made = sem("same_made")
        batch_made = sem("batch_made")
        mask_loaded = sem("mask_loaded")
        router_loaded = sem("router_loaded")
        x_loaded = [sem(f"x_loaded{u}") for u in range(4)]
        ctx_loaded = [sem(f"ctx_loaded{u}") for u in range(4)]
        w_loaded = [[sem(f"w_loaded{half}{u}") for u in range(2)] for half in range(2)]
        rest_loaded = [sem(f"rest_loaded{u}") for u in range(2)]
        w_hi_done = sem("w_hi_done")
        w_lo_done = sem("w_lo_done")
        rest_hi_done = sem("rest_hi_done")
        rest_lo_done = sem("rest_lo_done")
        valid_done = sem("valid_done")
        mask_copied = sem("mask_copied")
        bias_done = sem("bias_done")
        bias_ready = sem("bias_ready")
        bn1_done = sem("bn1_done")
        mv1_done = sem("mv1_done")
        xn_done = sem("xn_done")
        x_turned = sem("x_turned")
        c_turned = sem("c_turned")
        xt_ready = sem("xt_ready")
        ct_ready = sem("ct_ready")
        scored = sem("scored")
        top_done = sem("top_done")
        neg_done = sem("neg_done")
        exp_done = sem("exp_done")
        inv_done = sem("inv_done")
        factor_done = sem("factor_done")
        p_turned = sem("p_turned")
        pt_ready = sem("pt_ready")
        read_out = sem("read_out")
        x1_done = sem("x1_done")
        x1_stored = sem("x1_stored")
        zeros_made = sem("zeros_made")
        pads_stored = sem("pads_stored")
        bn2_done = sem("bn2_done")
        mv2_done = sem("mv2_done")
        var_done = sem("var_done")
        rstd_done = sem("rstd_done")
        xn2_done = sem("xn2_done")
        xn2_stored = [sem(f"xn2_stored{u}") for u in range(2)]
        x2_turned = sem("x2_turned")
        x2t_ready = sem("x2t_ready")
        routed = sem("routed")
        sort_step = sem("sort_step")
        hot16_done = sem("hot16_done")
        totaled = sem("totaled")
        totals_done = sem("totals_done")
        ranked = sem("ranked")
        gap_done = sem("gap_done")
        exp_d_done = sem("exp_d_done")
        slot_hl_done = sem("slot_hl_done")
        hot_val_done = sem("hot_val_done")
        hot_val_pool = sem("hot_val_pool")
        hot_val_act = sem("hot_val_act")
        gate_done = sem("gate_done")
        split_step = sem("split_step")
        rows_done = sem("rows_done")
        hot_row_done = sem("hot_row_done")
        hot_blk_done = sem("hot_blk_done")
        inverted = sem("inverted")
        slot_token_done = sem("slot_token_done")
        blk_done = sem("blk_done")
        gate_slot_done = sem("gate_slot_done")
        idx_done = sem("idx_done")
        gathered = [sem(f"gathered{u}") for u in range(2)]
        g_turned = sem("g_turned")
        g_hi = sem("g_hi")
        g_lo = sem("g_lo")
        gate_up = sem("gate_up")
        silu_done = sem("silu_done")
        hid_done = sem("hid_done")
        h_turned = sem("h_turned")
        h_hi = sem("h_hi")
        h_lo = sem("h_lo")
        down = sem("down")
        y_done = sem("y_done")
        idx_out_done = sem("idx_out_done")
        scattered = [sem(f"scattered{u}") for u in range(2)]
        waits_alone = sem("waits_alone")

        block = ctx.enter_context(nc.Block())

        def over(eng, step, count, steps, ahead, behind):
            rounds = (count - 4 - ahead) // steps
            for i in range(-ahead, 4):
                step(0, i)
            with eng.Fori(0, rounds) as r:
                for u in range(4, 4 + steps):
                    step(r, u)
            for i in range(4 + steps * rounds, count + behind):
                step(0, i)

        def over_batches(eng, step, ahead, behind):
            over(eng, step, B, 4, ahead, behind)

        def over_blocks(eng, step, ahead, behind):
            over(eng, step, NBLK, STEPS, ahead, behind)

        def looped(r):
            return not isinstance(r, int)

        def on(r, u, shift):
            return looped(r) or 0 <= u + shift < B

        def has(r, u, shift):
            return looped(r) or 0 <= u + shift < NBLK

        def at(r, u, i):
            return not looped(r) and u == i

        def wait_alone(eng, signal, value):
            eng.wait_ge(signal, value)
            eng.sem_inc(waits_alone, 1)

        quarters = [slice(q * NA // 4, (q + 1) * NA // 4) for q in range(4)]

        def hot_times(eng, k, value, n):
            return eng.tensor_tensor(hot_val[:, n, k, :], hot_blk[:, n, :],
                                     value.unsqueeze(2).to_broadcast([P, n.stop - n.start, NBLK]), ALU.mult)

        @block.sync
        def _(sp):
            def batch(r, u):
                i = 4 * r + u
                if on(r, u, 4):
                    if on(r, u, 0):
                        sp.wait_ge(bn1_done, i + 1)
                    sp.dma_start(x1[:, i + 4, :], x[i + 4]).then_inc(x_loaded[u % 4], 16)
                if on(r, u, 3):
                    if on(r, u, -1):
                        sp.wait_ge(read_out, i)
                    sp.dma_start(ctx_in[:, (u + 3) % 4, :], ctx_tokens[i + 3]).then_inc(ctx_loaded[(u + 3) % 4], 16)
                if at(r, u, -3):
                    sp.dma_start(mask_words[:, :, :], mask.partition_broadcast(P)).then_inc(mask_loaded, 16)
                    sp.dma_start(router_w[:, :, :], router_t).then_inc(router_loaded, 16)
                if on(r, u, 2):
                    for half in range(2):
                        if on(r, u, 0):
                            sp.wait_ge(w_lo_done, 2 * i + half + 1)
                        piece = slice(half * WHALF, (half + 1) * WHALF)
                        sp.dma_start(w_stage[:, u % 2, piece],
                                     weights[i + 2, :, piece]).then_inc(w_loaded[half][u % 2], 16)
                    if on(r, u, 0):
                        sp.wait_ge(rest_lo_done, i + 1)
                    sp.dma_start(rest_stage[:, u % 2, :], rest_weights[i + 2]).then_inc(rest_loaded[u % 2], 16)
                if at(r, u, -1):
                    sp.wait_ge(zeros_made, 1)
                    sp.dma_start(xn2_rows[T:T + P, :], xn2[:, 1, :]).then_inc(pads_stored, 16)
                    sp.dma_start(out[T:T + P, :], xn2[:, 1, :]).then_inc(pads_stored, 16)
                if on(r, u, -2):
                    sp.wait_ge(xn2_done, i - 1)
                    sp.dma_start(xn2_rows[bass.ds((i - 2) * P, P), :],
                                 xn2[:, u % 2, :]).then_inc(xn2_stored[u % 2], 16)

            over_batches(sp, batch, 4, 2)

            sp.wait_ge(x1_done, B)
            for i in range(0, B, 4):
                sp.dma_start(out[i * P:(i + 4) * P, :].rearrange("(b p) d -> p b d", p=P),
                             x1[:, i:i + 4, :]).then_inc(x1_stored, 16)
            sp.wait_ge(x1_stored, 16 * (B // 4))
            sp.wait_ge(scattered[0], 16 * ((NBLK + 1) // 2))
            sp.wait_ge(scattered[1], 16 * (NBLK // 2))

        @block.gpsimd
        def _(pool):
            g = nc.gpsimd
            g.memset(minus_half[:, :], -0.5)
            g.memset(eps_col[:, :], EPS).then_inc(const_made, 1)
            g.memset(ident[:, :], 0.0).then_inc(const_made, 1)
            pool.wait_ge(const_made, 2)
            g.affine_select(out=ident[:, :], in_=ident[:, :], compare_op=ALU.not_equal, fill=1.0, base=0,
                            pattern=[[-1, P]], channel_multiplier=1).then_inc(const_made, 1)
            g.memset(xn2[:, 1, :], 0.0).then_inc(zeros_made, 1)

            def batch(r, u):
                i = 4 * r + u
                if on(r, u, 0):
                    pool.wait_ge(w_hi_done, 2 * i + 1)
                    lower(i, u, 0).then_inc(w_lo_done, 1)
                if on(r, u, 2) or on(r, u, -2):
                    both = slice(0 if on(r, u, 2) else 1, 2 if on(r, u, -2) else 1)
                    if on(r, u, 2):
                        pool.wait_ge(mv1_done, i + 3)
                    if on(r, u, -2):
                        pool.wait_ge(mv2_done, i - 1)
                    g.tensor_tensor(var[:, u % 2, both], mv[:, u % 2, both, 1], eps_col[:, both],
                                    ALU.add).then_inc(var_done, 1)
                    pool.wait_ge(var_done, i + 3)
                    if on(r, u, 1):
                        pool.wait_ge(xn_done, i + 2)
                    if on(r, u, -3):
                        pool.wait_ge(xn2_done, i - 2)
                    g.tensor_tensor(rstd[:, both], var[:, u % 2, both], minus_half[:, both],
                                    ALU.pow).then_inc(rstd_done, 1)
                if on(r, u, 0):
                    if at(r, u, 0):
                        pool.wait_ge(valid_done, 2)
                    if on(r, u, -2):
                        pool.wait_ge(x1_done, i - 1)
                    pool.wait_ge(inv_done, i + 1)
                    g.tensor_tensor(factor[:, u % 2, :], inv_p[:, u % 2, :], valid[:, bass.ds(i, 1)],
                                    ALU.mult).then_inc(factor_done, 1)
                    pool.wait_ge(w_hi_done, 2 * i + 2)
                    lower(i, u, 1).then_inc(w_lo_done, 1)

            def lower(i, u, half):
                piece = bass.ds(i * WCH + half * WHALF, WHALF)
                return g.tensor_tensor(w_lo[:, piece], w_stage[:, u % 2, half * WHALF:(half + 1) * WHALF],
                                       w_hi[:, piece].bitcast(F32), ALU.subtract)

            def sort_constants():
                g.memset(ones16[:, :], 1.0).then_inc(const_made, 1)
                g.iota(row_iota[:, :], [[1, P]], base=0, channel_multiplier=0,
                       allow_small_or_imprecise_dtypes=True).then_inc(const_made, 1)
                g.iota(blk_iota[:, :], [[1, NBLK]], base=0, channel_multiplier=0,
                       allow_small_or_imprecise_dtypes=True).then_inc(const_made, 1)
                g.iota(batch_off[:, :, :], [[0, TOP_K], [P, B]], base=-T, channel_multiplier=0,
                       allow_small_or_imprecise_dtypes=True).then_inc(const_made, 1)
                g.iota(pad_token[:, :], [[0, 1]], base=T, channel_multiplier=1,
                       allow_small_or_imprecise_dtypes=True).then_inc(const_made, 1)
                g.iota(row_id[:, :], [[0, 1]], base=0, channel_multiplier=1,
                       allow_small_or_imprecise_dtypes=True).then_inc(const_made, 1)
                g.iota(expert_iota[:, :, :], [[0, B], [1, E]], base=0, channel_multiplier=0,
                       allow_small_or_imprecise_dtypes=True).then_inc(const_made, 1)
                g.memset(before_expert[:, :, :], 1.0).then_inc(const_made, 1)
                pool.wait_ge(const_made, 11)
                g.affine_select(out=before_expert[:, :, :], in_=before_expert[:, :, :], compare_op=ALU.is_gt,
                                fill=0.0, base=0, pattern=[[1, E], [-1, E]],
                                channel_multiplier=0).then_inc(const_made, 1)
                g.affine_select(out=before_token[:, :], in_=ones16[:, :], compare_op=ALU.is_gt,
                                fill=0.0, base=0, pattern=[[1, P]],
                                channel_multiplier=-1).then_inc(const_made, 1)
                pool.wait_ge(batch_made, 1)
                g.affine_select(out=before_batch[:, :, :], in_=before_batch[:, :, :], compare_op=ALU.is_gt,
                                fill=0.0, base=0, pattern=[[E, B], [0, E]],
                                channel_multiplier=-1).then_inc(batch_made, 1)

            sort_constants()
            over_batches(pool, batch, 2, 3)

            def then(ins):
                ins.then_inc(split_step, 1)
                split[0] += 1
                pool.wait_ge(split_step, split[0])

            split = [0]
            pool.wait_ge(gate_done, 1)
            then(g.tensor_copy(gate_part[:, 0, :], gate[:, :]))
            then(g.tensor_tensor(gate_rest[:, 0, :], gate[:, :], gate_part[:, 0, :], ALU.subtract))
            then(g.tensor_copy(gate_part[:, 1, :], gate_rest[:, 0, :]))
            then(g.tensor_tensor(gate_rest[:, 1, :], gate_rest[:, 0, :], gate_part[:, 1, :], ALU.subtract))
            then(g.tensor_copy(gate_part[:, 2, :], gate_rest[:, 1, :]))
            for q, n in enumerate(quarters):
                pool.wait_ge(hot_blk_done, q // 2 + 1)
                for k in (2, 3, 4) if q < 3 else (3, 4):
                    hot = hot_times(g, k, gate_part[:, k - 2, n], n)
                hot.then_inc(hot_val_pool, 1)

            pool.wait_ge(slot_token_done, 1)
            pool.wait_ge(pads_stored, 32)
            pool.wait_ge(xn2_stored[0], 16 * (B // 2))
            pool.wait_ge(xn2_stored[1], 16 * (B // 2))

            def blocks(r, u):
                b = STEPS * r + u
                if has(r, u, 3):
                    v = u + 3
                    if has(r, u, 1):
                        wait_alone(pool, gathered[v % 2], 8 * STEPS * r + 16 * ((v - 2) // 2 + 1))
                    g.tensor_copy(idx[v % 2][:, :], slot_token[:, bass.ds(b + 3, 1)]).then_inc(idx_done, 1)
                if has(r, u, -2):
                    v = u - 2
                    if has(r, u, -4):
                        wait_alone(pool, scattered[v % 2], 8 * STEPS * r + 16 * ((v - 2) // 2 + 1))
                    g.tensor_copy(idx_out[v % 2][:, :], slot_token[:, bass.ds(b - 2, 1)]).then_inc(idx_out_done, 1)
                if has(r, u, 3):
                    v = u + 3
                    if has(r, u, 1):
                        pool.wait_ge(g_turned, b + 2)
                    wait_alone(pool, idx_done, b + 4)
                    g.indirect_dma_start(out=xg[:, v % 2, :], out_offset=None, in_=xn2_rows[:, :],
                                         in_offset=bass.IndirectOffsetOnAxis(ap=idx[v % 2][:, 0:1], axis=0)
                                         ).then_inc(gathered[v % 2], 16)
                if has(r, u, -2):
                    v = u - 2
                    pool.wait_ge(idx_out_done, b - 1)
                    pool.wait_ge(y_done, b - 1)
                    if has(r, u, -3):
                        wait_alone(pool, scattered[(v - 1) % 2], 8 * STEPS * r + 16 * ((v - 1) // 2 + 1))
                    else:
                        wait_alone(pool, x1_stored, 16 * (B // 4))
                    g.indirect_dma_start(out=out[:, :],
                                         out_offset=bass.IndirectOffsetOnAxis(ap=idx_out[v % 2][:, 0:1], axis=0),
                                         in_=y[:, v % 2, :], in_offset=None,
                                         compute_op=ALU.add).then_inc(scattered[v % 2], 16)

            over_blocks(pool, blocks, 3, 2)

        @block.tensor
        def _(pe):
            t = nc.tensor
            pe.wait_ge(const_made, 3)
            pe.wait_ge(router_loaded, 16)

            def batch(r, u):
                i = 4 * r + u
                if on(r, u, -1):
                    pe.wait_ge(exp_done, i)
                    if on(r, u, -2):
                        pe.wait_ge(pt_ready, i - 1)
                    t.transpose(ps_p[:, 0:P], probs[:, :], ident[:, :]).then_inc(p_turned, 1)
                if on(r, u, 0):
                    pe.wait_ge(xt_ready, i + 1)
                    pe.wait_ge(ct_ready, i + 1)
                    if on(r, u, -1):
                        pe.wait_ge(top_done, i)
                    for k in range(KD):
                        mm = t.matmul(ps_s[:, 0:P], xn_t[:, k, :], ctx_t[:, k, :],
                                      start=(k == 0), stop=(k == KD - 1))
                    mm.then_inc(scored, 1)
                if on(r, u, 1):
                    v = u + 1
                    pe.wait_ge(ctx_loaded[v % 4], 16 * r + 16 * (v // 4 + 1))
                    for k in range(KD):
                        mm = t.transpose(ps_c[:, k, :], ctx_in[:, v % 4, k * P:(k + 1) * P], ident[:, :])
                    mm.then_inc(c_turned, 1)
                    pe.wait_ge(xn_done, i + 2)
                    for k in range(KD):
                        mm = t.transpose(ps_x[:, k, :], xn[:, k * P:(k + 1) * P], ident[:, :])
                    mm.then_inc(x_turned, 1)
                if on(r, u, -4):
                    pe.wait_ge(x2t_ready, i - 3)
                    to = ps_c[:, 0, :] if not looped(r) and i - 4 >= EARLY else ps_router
                    for k in range(KD):
                        mm = t.matmul(to[:, bass.ds((i - 4) * E, E)], xn2_t[:, k, :], router_w[:, k, :],
                                      start=(k == 0), stop=(k == KD - 1))
                    mm.then_inc(routed, 1)
                if on(r, u, -3):
                    pe.wait_ge(xn2_done, i - 2)
                    for k in range(KD):
                        mm = t.transpose(ps_x2[:, k, :], xn2[:, (u - 3) % 2, k * P:(k + 1) * P], ident[:, :])
                    mm.then_inc(x2_turned, 1)
                if on(r, u, -1):
                    pe.wait_ge(pt_ready, i)
                    if on(r, u, -3):
                        pe.wait_ge(x1_done, i - 2)
                    t.matmul(ps_r[:, (u - 1) % 2, :], probs_t[:, :], ctx_in[:, (u - 1) % 4, :],
                             start=True, stop=True).then_inc(read_out, 1)

            over_batches(pe, batch, 1, 4)

            pe.wait_ge(hot16_done, 1)
            t.matmul(ps_total[:, 0:1], hot16.rearrange("p b e -> p (b e)"), ones16[:, 0:1],
                     start=True, stop=True).then_inc(totaled, 1)
            pe.wait_ge(totals_done, 1)
            pe.wait_ge(batch_made, 2)
            t.matmul(ps_count[:, 0:E], totals[:, :], same_expert[:, :], start=True, stop=True).then_inc(ranked, 1)
            pe.wait_ge(const_made, 13)
            t.matmul(ps_rank[:, 0:P], before_token[:, :], hot16.rearrange("p b e -> p (b e)"),
                     start=True, stop=False)
            t.matmul(ps_rank[:, 0:P], totals[:, :], before_batch.rearrange("p b e -> p (b e)"),
                     start=False, stop=True).then_inc(ranked, 1)
            for n in range(NA):
                pe.wait_ge(hot_row_done, n + 1)
                pe.wait_ge(hot_val_act, n + 1)
                if n % (NA // 2) == 0:
                    pe.wait_ge(hot_val_done, n // (NA // 2) + 1)
                if n % (NA // 4) == 0:
                    pe.wait_ge(hot_val_pool, n // (NA // 4) + 1)
                mm = t.matmul(ps_inv[:, 0:VALUES * NBLK], hot_row[:, n, :],
                              hot_val[:, n, :, :].rearrange("p v b -> p (v b)"),
                              start=(n == 0), stop=(n == NA - 1))
            mm.then_inc(inverted, 1)

            pe.wait_ge(w_hi_done, 2 * B)
            pe.wait_ge(w_lo_done, 2 * B)
            pe.wait_ge(rest_lo_done, B)
            pe.wait_ge(blk_done, 1)
            pe.wait_ge(slot_token_done, 1)

            def experts_of(b):
                pair = pe.value_load(blk_experts[0:1, bass.ds(b, 1)], min_val=0, max_val=E * E - 1)
                return pair // E, pair % E

            def turn_hidden(r, u):
                b = STEPS * r + u
                v = u - 1
                pe.wait_ge(hid_done, b)
                if has(r, u, -3):
                    pe.wait_ge(h_hi, b - 2)
                    pe.wait_ge(h_lo, b - 2)
                for half in range(2):
                    mm = t.transpose(ps_h[:, v % 2, half * P:(half + 1) * P], hid[:, v % 2, half, :], ident[:, :])
                mm.then_inc(h_turned, 1)

            def blocks(r, u):
                b = STEPS * r + u
                if has(r, u, 0) or has(r, u, -1):
                    e, e_down = experts_of(b)
                if has(r, u, 0):
                    pe.wait_ge(g_hi, b + 1)
                    if has(r, u, -2):
                        pe.wait_ge(hid_done, b - 1)
                for k in range(KD):
                    if k == KD // 2 and has(r, u, -1):
                        turn_hidden(r, u)
                    for w in (w_hi, w_lo):
                        if has(r, u, 0):
                            t.matmul(ps_gu[:, u % 2, 0:2 * F], xg_hi[:, u % 2, k, :],
                                     w[:, bass.ds(e * WGU + k * 2 * F, 2 * F)],
                                     start=(k == 0 and w is w_hi), stop=False)
                if has(r, u, 0):
                    pe.wait_ge(g_lo, b + 1)
                    for k in range(KD):
                        mm = t.matmul(ps_gu[:, u % 2, 0:2 * F], xg_lo[:, u % 2, k, :],
                                      w_hi[:, bass.ds(e * WGU + k * 2 * F, 2 * F)],
                                      start=False, stop=(k == KD - 1))
                    mm.then_inc(gate_up, 1)
                if has(r, u, -1):
                    v = u - 1
                    pe.wait_ge(h_hi, b)
                    if has(r, u, -3):
                        pe.wait_ge(y_done, b - 2)
                    first = bass.ds(e_down * D + WDOWN, D)
                    rest = bass.ds(e_down * D, D)
                    products = (
                        (hid_hi[:, v % 2, 0, :], w_hi[:, first]),
                        (hid_hi[:, v % 2, 0, :], w_lo[:, first]),
                        (hid_hi[:, v % 2, 1, :], w_rest[:, rest]),
                        (hid_lo[:, v % 2, 0, :], w_hi[:, first]),
                        (hid_lo[0:FB, v % 2, 1, :], w_rest[0:FB, rest]),
                    )
                    for n, (lhs, w) in enumerate(products):
                        if n == 3:
                            pe.wait_ge(h_lo, b)
                        mm = t.matmul(ps_y[:, v % 2, :], lhs, w, start=(n == 0), stop=(n == len(products) - 1))
                    mm.then_inc(down, 1)
                if has(r, u, 2):
                    v = u + 2
                    pe.wait_ge(gathered[v % 2], 8 * STEPS * r + 16 * (v // 2 + 1))
                    if has(r, u, 0):
                        pe.wait_ge(g_lo, b + 1)
                        pe.wait_ge(g_hi, b + 1)
                    for k in range(KD):
                        mm = t.transpose(ps_xg[:, v % 2, k, :], xg[:, v % 2, k * P:(k + 1) * P], ident[:, :])
                    mm.then_inc(g_turned, 1)

            over_blocks(pe, blocks, 2, 1)

        @block.scalar
        def _(act):
            s = nc.scalar

            def batch(r, u):
                i = 4 * r + u
                if on(r, u, -1):
                    act.wait_ge(p_turned, i)
                    if on(r, u, -2):
                        act.wait_ge(read_out, i - 1)
                    s.activation(probs_t[:, :], ps_p[:, 0:P], ACT.Copy).then_inc(pt_ready, 1)
                if on(r, u, 0):
                    for half in range(2):
                        act.wait_ge(w_loaded[half][u % 2], 32 * r + 16 * (u // 2 + 1))
                        s.activation(w_hi[:, bass.ds(i * WCH + half * WHALF, WHALF)],
                                     w_stage[:, u % 2, half * WHALF:(half + 1) * WHALF],
                                     ACT.Copy).then_inc(w_hi_done, 1)
                    act.wait_ge(rest_loaded[u % 2], 32 * r + 16 * (u // 2 + 1))
                    s.activation(w_rest[0:FB, bass.ds(i * WREST, WREST)], rest_stage[:, u % 2, :],
                                 ACT.Copy).then_inc(rest_hi_done, 1)
                    act.wait_ge(neg_done, i + 1)
                    if on(r, u, -1):
                        act.wait_ge(p_turned, i)
                    s.activation(probs[:, :], scores[:, :], ACT.Exp, bias=neg_top[:, :],
                                 accum_out=psum_p[:, :]).then_inc(exp_done, 1)
                if on(r, u, 1):
                    act.wait_ge(c_turned, i + 2)
                    if on(r, u, 0):
                        act.wait_ge(scored, i + 1)
                    s.activation(ctx_t[:, :, :], ps_c[:, :, :], ACT.Copy).then_inc(ct_ready, 1)
                    act.wait_ge(x_turned, i + 2)
                    s.activation(xn_t[:, :, :], ps_x[:, :, :], ACT.Copy).then_inc(xt_ready, 1)
                    if at(r, u, -1):
                        act.wait_ge(bias_done, 1)
                    s.activation(bias_now[:, (u + 1) % 2, :],
                                 bias[:, bass.ds(i + 1, 1), :].rearrange("p o m -> p (o m)"),
                                 ACT.Copy).then_inc(bias_ready, 1)
                if on(r, u, -3):
                    act.wait_ge(x2_turned, i - 2)
                    if on(r, u, -4):
                        act.wait_ge(routed, i - 3)
                    s.activation(xn2_t[:, :, :], ps_x2[:, :, :], ACT.Copy).then_inc(x2t_ready, 1)

            over_batches(act, batch, 1, 3)

            act.wait_ge(gap_done, 1)
            s.activation(exp_d[:, :], gap[:, :], ACT.Exp).then_inc(exp_d_done, 1)
            act.wait_ge(const_made, 1)
            s.activation(silu_probe[:, :], eps_col[:, 0:1], ACT.Silu)
            act.wait_ge(rows_done, 1)
            for n in range(NA):
                if n % (NA // 2) == 0:
                    act.wait_ge(hot_blk_done, n // (NA // 2) + 1)
                s.activation(hot_val[:, n, 1, :], hot_blk[:, n, :], ACT.Copy,
                             scale=row_diff[:, n:n + 1]).then_inc(hot_val_act, 1)
            act.wait_ge(gate_slot_done, 1)

            def blocks(r, u):
                b = STEPS * r + u
                if has(r, u, -1):
                    v = u - 1
                    act.wait_ge(h_turned, b)
                    if has(r, u, -3):
                        act.wait_ge(down, b - 2)
                    s.activation(hid_hi[:, v % 2, :, :], ps_h[:, v % 2, 0:2 * P],
                                 ACT.Copy).then_inc(h_hi, 1)
                if has(r, u, 0):
                    act.wait_ge(gate_up, b + 1)
                    if has(r, u, -2):
                        act.wait_ge(hid_done, b - 1)
                    s.activation(act_g[:, u % 2, :], ps_gu[:, u % 2, 0:F], ACT.Silu).then_inc(silu_done, 1)
                if has(r, u, 2):
                    v = u + 2
                    act.wait_ge(g_turned, b + 3)
                    if has(r, u, 0):
                        act.wait_ge(gate_up, b + 1)
                    s.activation(xg_hi[:, v % 2, :, :], ps_xg[:, v % 2, :, :], ACT.Copy).then_inc(g_hi, 1)
                if has(r, u, -1):
                    v = u - 1
                    act.wait_ge(down, b)
                    if has(r, u, -3):
                        act.wait_ge(scattered[v % 2], 8 * STEPS * r + 16 * ((u - 3) // 2 + 1))
                    s.activation(y[:, v % 2, :], ps_y[:, v % 2, :], ACT.Copy,
                                 scale=gate_slot[:, bass.ds(b - 1, 1)]).then_inc(y_done, 1)

            over_blocks(act, blocks, 2, 1)

        @block.vector
        def _(dve):
            v_ = nc.vector
            dve.wait_ge(const_made, 3)
            with nc.allow_low_precision("zeros and ones"):
                v_.tensor_reduce(same_expert[:, :], ident.rearrange("p (b e) -> p e b", e=E), AX.X,
                                 ALU.add).then_inc(same_made, 1)
            dve.wait_ge(same_made, 1)
            v_.tensor_copy(before_batch[:, :, :],
                           same_expert[:, :].unsqueeze(1).to_broadcast([P, B, E])).then_inc(batch_made, 1)

            def add_readout(i, u):
                dve.wait_ge(factor_done, i - 1)
                dve.wait_ge(read_out, i - 1)
                v_.scalar_tensor_tensor(x1[:, i - 2, :], ps_r[:, u % 2, :], factor[:, u % 2, :],
                                        x1[:, i - 2, :], ALU.mult, ALU.add).then_inc(x1_done, 1)

            def batch(r, u):
                i = 4 * r + u
                last = at(r, u, B + 1)
                if on(r, u, -2) and not last:
                    add_readout(i, u)
                if on(r, u, 0):
                    if on(r, u, -1):
                        dve.wait_ge(exp_done, i)
                    dve.wait_ge(bias_ready, i + 1)
                    wait_alone(dve, scored, i + 1)
                    v_.tensor_tensor_reduce(scores[:, :], ps_s[:, 0:P], bias_now[:, u % 2, :], SCALE, LOWEST,
                                            ALU.add, ALU.max, top[:, :]).then_inc(top_done, 1)
                if on(r, u, -2):
                    wait_alone(dve, x1_done, i - 1)
                    v_.bn_stats(bn_b[:, :], x1[:, i - 2, :]).then_inc(bn2_done, 1)
                if on(r, u, 0):
                    dve.wait_ge(top_done, i + 1)
                    v_.tensor_scalar(neg_top[:, :], top[:, :], -1.0, None, ALU.mult).then_inc(neg_done, 1)
                if on(r, u, -2):
                    wait_alone(dve, bn2_done, i - 1)
                    v_.bn_aggr(mv[:, u % 2, 1, :], bn_b[:, :]).then_inc(mv2_done, 1)
                if on(r, u, 3):
                    v = u + 3
                    wait_alone(dve, x_loaded[v % 4], 16 * r + 16 * (v // 4 + 1))
                    v_.bn_stats(bn_a[:, (u + 3) % 2, :], x1[:, i + 3, :]).then_inc(bn1_done, 1)
                if on(r, u, 0):
                    dve.wait_ge(exp_done, i + 1)
                    v_.reciprocal(inv_p[:, u % 2, :], psum_p[:, :]).then_inc(inv_done, 1)
                    dve.wait_ge(rest_hi_done, i + 1)
                    v_.tensor_tensor(w_rest[FB:P, bass.ds(i * WREST, WREST)], rest_stage[:, u % 2, :],
                                     w_rest[0:FB, bass.ds(i * WREST, WREST)].bitcast(F32),
                                     ALU.subtract).then_inc(rest_lo_done, 1)
                if on(r, u, 3):
                    wait_alone(dve, bn1_done, i + 4)
                    v_.bn_aggr(mv[:, (u + 3) % 2, 0, :], bn_a[:, (u + 3) % 2, :]).then_inc(mv1_done, 1)
                if on(r, u, 2):
                    dve.wait_ge(rstd_done, i + 3)
                    if on(r, u, 1):
                        dve.wait_ge(x_turned, i + 2)
                    v_.tensor_scalar(xn[:, :], x1[:, i + 2, :], mv[:, u % 2, 0, 0:1], rstd[:, 0:1],
                                     ALU.subtract, ALU.mult).then_inc(xn_done, 1)
                if at(r, u, -2):
                    dve.wait_ge(mask_loaded, 16)
                    v_.tensor_copy(bias[:, :, :], mask_u8).then_inc(mask_copied, 1)
                    v_.tensor_reduce(valid[:, :], mask_words[:, :, :], AX.X, ALU.max).then_inc(valid_done, 1)
                    dve.wait_ge(mask_copied, 1)
                    v_.tensor_scalar(bias[:, :, :], bias[:, :, :], -MASKED / SCALE,
                                     MASKED / SCALE, ALU.mult, ALU.add).then_inc(bias_done, 1)
                    dve.wait_ge(valid_done, 1)
                    v_.tensor_scalar(valid[:, :], valid[:, :], 1.0, None, ALU.min).then_inc(valid_done, 1)
                    dve.wait_ge(valid_done, 2)
                if at(r, u, B):
                    add_readout(i + 1, u + 1)
                if on(r, u, -2):
                    dve.wait_ge(rstd_done, i + 3)
                    if at(r, u, 3):
                        dve.wait_ge(pads_stored, 32)
                    if on(r, u, -4):
                        dve.wait_ge(x2_turned, i - 3)
                        dve.wait_ge(xn2_stored[u % 2], 32 * r + 16 * ((u - 4) // 2 + 1))
                    v_.tensor_scalar(xn2[:, u % 2, :], x1[:, i - 2, :], mv[:, u % 2, 1, 0:1],
                                     rstd[:, 1:2], ALU.subtract, ALU.mult).then_inc(xn2_done, 1)

            over_batches(dve, batch, 3, 2)

            chain = [0]

            def then(ins):
                chain[0] += 1
                ins.then_inc(sort_step, 1)
                dve.wait_ge(sort_step, chain[0])

            def choose(ps_scores, first, last):
                n = slice(first, last)
                router_scores = ps_scores.rearrange("p (b e) -> p b e", e=E)[:, n, :]

                def over_e(m):
                    return m[:, n].unsqueeze(2).to_broadcast([P, last - first, E])

                def best(scores, top, first_of, hot):
                    then(v_.tensor_reduce(top[:, n], scores, AX.X, ALU.max))
                    then(v_.tensor_tensor(not_top[:, n, :], scores, over_e(top), ALU.is_lt))
                    then(v_.scalar_tensor_tensor(cand[:, n, :], not_top[:, n, :], float(E), expert_iota[:, n, :],
                                                 ALU.mult, ALU.add))
                    then(v_.tensor_reduce(first_of[:, n], cand[:, n, :], AX.X, ALU.min))
                    then(v_.tensor_tensor(hot[:, n, :], expert_iota[:, n, :], over_e(first_of), ALU.is_equal))

                best(router_scores, top1, first1, hot1)
                then(v_.scalar_tensor_tensor(rs2[:, n, :], hot1[:, n, :], LOWEST, router_scores,
                                             ALU.mult, ALU.add))
                best(rs2[:, n, :], top2, first2, hot2)

            dve.wait_ge(const_made, 13)
            dve.wait_ge(routed, EARLY)
            choose(ps_router, 0, EARLY)
            dve.wait_ge(routed, B)
            choose(ps_c[:, 0, :], EARLY, B)
            dve.wait_ge(xn2_stored[0], 16 * (B // 2))
            dve.wait_ge(xn2_stored[1], 16 * (B // 2))
            dve.wait_ge(batch_made, 2)
            v_.tensor_tensor(hot16[:, :, :], hot1[:, :, :], hot2[:, :, :], ALU.add).then_inc(hot16_done, 1)
            v_.tensor_tensor(gap[:, :], top2[:, :], top1[:, :], ALU.subtract).then_inc(gap_done, 1)
            dve.wait_ge(totaled, 1)
            v_.tensor_scalar(totals[:, :], ones16[:, :], ps_total[:, 0:1], None, ALU.mult).then_inc(totals_done, 1)
            dve.wait_ge(exp_d_done, 1)
            then(v_.tensor_scalar(denom[:, :], exp_d[:, :], 1.0, None, ALU.add))
            then(v_.reciprocal(gate[:, 0:B], denom[:, :]))
            v_.tensor_tensor(gate[:, B:NA], gate[:, 0:B], exp_d[:, :], ALU.mult).then_inc(gate_done, 1)
            dve.wait_ge(ranked, 1)
            then(v_.tensor_scalar(blocks_i[:, 0, :], ps_count[:, 0:E], float(P - 1), None, ALU.add))
            then(v_.tensor_scalar(blocks_i[:, 1, :], blocks_i[:, 0, :], 7, None, ALU.logical_shift_right))
            then(v_.tensor_copy(blocks_f[:, :], blocks_i[:, 1, :]))
            then(v_.tensor_tensor(start_terms[:, :, :], before_expert[:, :, :],
                                  blocks_f[:, :].unsqueeze(1).to_broadcast([P, E, E]), ALU.mult))
            then(v_.tensor_reduce(start[:, :], start_terms[:, :, :], AX.X, ALU.add))
            dve.wait_ge(ranked, 2)
            then(v_.scalar_tensor_tensor(slot[:, :, :], start[:, :].unsqueeze(1).to_broadcast([P, B, E]), float(P),
                                         ps_rank[:, 0:P].rearrange("p (b e) -> p b e", e=E),
                                         ALU.mult, ALU.add))
            v_.tensor_tensor(picked[:, 0, :, :], hot1[:, :, :], slot[:, :, :], ALU.mult)
            then(v_.tensor_tensor(picked[:, 1, :, :], hot2[:, :, :], slot[:, :, :], ALU.mult))
            then(v_.tensor_reduce(slot_f[:, :], picked.rearrange("p k b e -> p (k b) e"), AX.X, ALU.add))
            then(v_.tensor_copy(slot_i[:, 0, :], slot_f[:, :]))
            v_.tensor_scalar(slot_i[:, 1, :], slot_i[:, 0, :], 7, None, ALU.logical_shift_right)
            then(v_.tensor_scalar(slot_i[:, 2, :], slot_i[:, 0, :], P - 1, None, ALU.bitwise_and))
            v_.tensor_copy(slot_blk[:, :], slot_i[:, 1, :])
            v_.tensor_copy(slot_hl[:, :, :], slot_i[:, 1:3, :]).then_inc(slot_hl_done, 1)
            dve.wait_ge(slot_hl_done, 1)
            halves = [slice(half * NA // 2, (half + 1) * NA // 2) for half in range(2)]
            for n in halves:
                v_.tensor_tensor(hot_blk[:, n, :], blk_iota[:, :].unsqueeze(1).to_broadcast([P, NA // 2, NBLK]),
                                 slot_blk[:, n].unsqueeze(2).to_broadcast([P, NA // 2, NBLK]),
                                 ALU.is_equal).then_inc(hot_blk_done, 1)
                if n.start == 0:
                    v_.tensor_scalar(row_diff[:, :], slot_hl[:, 1, :], -1.0, row_id[:, :],
                                     ALU.mult, ALU.add).then_inc(rows_done, 1)
            for half, n in enumerate(halves):
                dve.wait_ge(hot_blk_done, half + 1)
                hot = hot_times(v_, 0, batch_off.rearrange("p k b -> p (k b)")[:, n], n)
                if half == 1:
                    dve.wait_ge(split_step, 1)
                    hot = hot_times(v_, 2, gate_part[:, 0, quarters[3]], quarters[3])
                hot.then_inc(hot_val_done, 1)
                for row in range(n.start, n.stop):
                    v_.tensor_scalar(hot_row[:, row, :], row_iota[:, :], slot_hl[:, 1, row:row + 1], None,
                                     ALU.is_equal).then_inc(hot_row_done, 1)
            then(v_.tensor_tensor(begun[:, :, :], blk_iota[:, :].unsqueeze(2).to_broadcast([P, NBLK, E - 1]),
                                  start[:, 1:E].unsqueeze(1).to_broadcast([P, NBLK, E - 1]), ALU.is_ge))
            then(v_.memset(blk_f[:, :], 0.0))
            then(v_.tensor_reduce(blk_f[:, 1:NBLK + 1], begun[:, :, :], AX.X, ALU.add))
            v_.scalar_tensor_tensor(blk_experts[:, :], blk_f[:, 1:NBLK + 2], float(E), blk_f[:, 0:NBLK + 1],
                                    ALU.mult, ALU.add).then_inc(blk_done, 1)
            dve.wait_ge(inverted, 1)
            def part(k):
                return ps_inv[:, k * NBLK:(k + 1) * NBLK]

            then(v_.tensor_scalar(row_off[:, :], part(1), pad_token[:, :], None, ALU.add))
            v_.tensor_tensor(slot_token[:, :], part(0), row_off[:, :], ALU.add).then_inc(slot_token_done, 1)
            then(v_.tensor_copy(gate_low[:, :], part(4)))
            then(v_.tensor_tensor(gate_low[:, :], part(3), gate_low[:, :], ALU.add))
            v_.tensor_tensor(gate_slot[:, :], part(2), gate_low[:, :], ALU.add).then_inc(gate_slot_done, 1)

            def blocks(r, u):
                b = STEPS * r + u
                if has(r, u, -1):
                    v = u - 1
                    dve.wait_ge(h_hi, b)
                    v_.tensor_tensor(hid_lo[:, v % 2, :, :],
                                     ps_h[:, v % 2, 0:2 * P].rearrange("p (h t) -> p h t", h=2),
                                     hid_hi[:, v % 2, :, :].bitcast(F32), ALU.subtract).then_inc(h_lo, 1)
                if has(r, u, 0):
                    dve.wait_ge(silu_done, b + 1)
                    if has(r, u, -2):
                        dve.wait_ge(h_turned, b - 1)
                    v_.tensor_tensor(hid[:, u % 2, 0, :], act_g[:, u % 2, 0:P], ps_gu[:, u % 2, F:F + P],
                                     ALU.mult)
                    v_.tensor_tensor(hid[:, u % 2, 1, :].rearrange("p (h f) -> p h f", h=2),
                                     act_g[:, u % 2, P:F].unsqueeze(1).to_broadcast([P, 2, FB]),
                                     ps_gu[:, u % 2, F + P:2 * F].unsqueeze(1).to_broadcast([P, 2, FB]),
                                     ALU.mult).then_inc(hid_done, 1)
                if has(r, u, 2):
                    v = u + 2
                    dve.wait_ge(g_hi, b + 3)
                    v_.tensor_tensor(xg_lo[:, v % 2, :, :], ps_xg[:, v % 2, :, :],
                                     xg_hi[:, v % 2, :, :].bitcast(F32), ALU.subtract).then_inc(g_lo, 1)

            over_blocks(dve, blocks, 2, 1)


def kernel(x, ctx_2048, mask_BxS2_bk0, L0_ffn_w_gate_router, L0_ffn_w_gate_proj, L0_ffn_w_up_proj,
           L0_ffn_w_down_proj):
    import numpy as np
    import concourse.bacc as bacc
    from concourse import mybir as mb
    from concourse.bass_utils import run_bass_kernel_spmd

    P = 128
    x, ctx_2048 = np.asarray(x), np.asarray(ctx_2048)
    router, gate, up, down = (np.asarray(a) for a in (L0_ffn_w_gate_router, L0_ffn_w_gate_proj,
                                                      L0_ffn_w_up_proj, L0_ffn_w_down_proj))
    B, S, D = x.shape
    E, F, _ = gate.shape
    KD = D // P
    gu = np.concatenate([gate.transpose(0, 2, 1), up.transpose(0, 2, 1)], axis=2)
    gu = gu.reshape(E, KD, P, 2 * F).transpose(2, 0, 1, 3).reshape(P, -1)
    dn = down.transpose(0, 2, 1)
    first = dn[:, :P].transpose(1, 0, 2).reshape(P, -1)
    rest = dn[:, P:].transpose(1, 0, 2).reshape(F - P, B, -1).transpose(1, 0, 2)
    w = np.concatenate([gu, first], axis=1).reshape(P, B, -1).transpose(1, 0, 2)
    arrays = {
        "x": x,
        "ctx": ctx_2048,
        "mask": np.ascontiguousarray(mask_BxS2_bk0).view(np.int32),
        "router_t": router.transpose(1, 0).reshape(KD, P, E).transpose(1, 0, 2),
        "weights": w,
        "rest_weights": rest,
    }
    arrays = {k: np.ascontiguousarray(v) for k, v in arrays.items()}
    nc = bacc.Bacc("TRN2", target_bir_lowering=False, num_devices=1, dynamic_dma_scratch_size=4096)
    args = [nc.dram_tensor(k, v.shape, mb.dt.from_np(v.dtype), kind="ExternalInput").ap()
            for k, v in arrays.items()]
    out = nc.dram_tensor("out", (B * S + P, D), mb.dt.float32, kind="ExternalOutput").ap()
    xattn_moe_kernel(nc, *args, out)
    got = run_bass_kernel_spmd(nc, [arrays], core_ids=[0])
    return got.results[0]["out"][:B * S].reshape(B, S, D)
```
